# Optimizing a Trainium2 kernel written in Bass

```python
import numpy as np
import jax
import jax.numpy as jnp

def _softmax(x, axis=-1):
    return jax.nn.softmax(x, axis=axis)

def _gelu(x):
    return jax.nn.gelu(x, approximate=True)

def _silu(x):
    return jax.nn.silu(x)

def _sigmoid(x):
    return jax.nn.sigmoid(x)

def _layernorm(x, axis=-1, eps=1e-05):
    m = jnp.mean(x, axis=axis, keepdims=True)
    v = jnp.var(x, axis=axis, keepdims=True)
    return (x - m) / jnp.sqrt(v + eps)

def _scatter_add(tgt, idx, src, axis=0):
    return tgt.at[idx].add(src)

def _segment_sum(src, seg, n):
    return jax.ops.segment_sum(src, seg, n)
kernel_name = 'mk_cond_seq_d2_seqx_r4_0ed798'

def setup_inputs(seed: int=0):
    np.random.seed(seed)
    _w = jnp.asarray

    def _rec_inputs():
        import jax
        import jax.numpy as jnp
        _rk = jax.random.key(seed)
        x = -0.000125 + 0.9999 * jax.random.normal(jax.random.fold_in(_rk, 1), (8, 512, 256), jnp.float32)
        _lenS = 512 - jax.random.randint(jax.random.fold_in(_rk, 7), (8,), 0, max(1, 512 // 4) + 1, jnp.int32)
        _lenS2 = 512 - jax.random.randint(jax.random.fold_in(_rk, 8), (8,), 0, max(1, 512 // 4) + 1, jnp.int32)
        itok_B_0_15 = jax.random.randint(jax.random.fold_in(_rk, 11), (8,), 0, 16, jnp.int32)
        itok_B_34_63 = jax.random.randint(jax.random.fold_in(_rk, 13), (8,), 34, 64, jnp.int32)
        fside_Bx16xSxS_0 = -1.47943e-05 + 1.00017 * jax.random.normal(jax.random.fold_in(_rk, 14), (8, 16, 512, 512), jnp.float32)
        _validS = jnp.arange(512)[None, :] < _lenS[:, None]
        _validS2 = jnp.arange(512)[None, :] < _lenS2[:, None]
        _causal = jnp.tril(jnp.ones((512, 512), dtype=bool))
        mask_Bx1xSxS_bk0 = jnp.logical_not(jnp.broadcast_to(_validS[:, None, None, :], (8, 1, 512, 512)))
        return (x, itok_B_0_15, itok_B_34_63, fside_Bx16xSxS_0, mask_Bx1xSxS_bk0)
    x, itok_B_0_15, itok_B_34_63, fside_Bx16xSxS_0, mask_Bx1xSxS_bk0 = _rec_inputs()

    def _L0_cond_setup():
        import jax, jax.numpy as jnp
        import numpy as np
        B, S, D = (32, 256, 256)
        A = 64
        E = 16
        LN_EPS = 1e-05
        key = jax.random.key(seed)
        ks = jax.random.split(key, 10)
        s = lambda fan_in: 1.0 / np.sqrt(fan_in)
        return {'hidden_states': jax.random.normal(ks[0], (B, S, D), dtype=jnp.float32), 'domain_id': jax.random.randint(ks[1], (B,), 0, E, dtype=jnp.int64), 'down_W': jax.random.uniform(ks[2], (A, D), jnp.float32, -s(D), s(D)), 'down_b': jax.random.uniform(ks[3], (A,), jnp.float32, -s(D), s(D)), 'up_W': jax.random.uniform(ks[4], (D, A), jnp.float32, -s(A), s(A)), 'up_b': jax.random.uniform(ks[5], (D,), jnp.float32, -s(A), s(A)), 'expert_W': jax.random.uniform(ks[6], (E, A, A), jnp.float32, -s(A), s(A)), 'expert_b': jax.random.uniform(ks[7], (E, A), jnp.float32, -s(A), s(A)), 'domain_emb': jax.random.normal(ks[8], (E, A), dtype=jnp.float32), 'ln_gamma': jnp.ones((D,), jnp.float32), 'ln_beta': jnp.zeros((D,), jnp.float32)}
    _L0_cond_all = _L0_cond_setup()
    _L0_cond_in = {k: v for k, v in _L0_cond_all.items() if k in ('down_W', 'down_b', 'up_W', 'up_b', 'expert_W', 'expert_b', 'domain_emb', 'ln_gamma', 'ln_beta')}
    del _L0_cond_all

    def _L1_cond_setup():
        import jax, jax.numpy as jnp
        import numpy as np
        import math
        D_MODEL = 256
        N_HEAD = 16
        HEAD_DIM = D_MODEL // N_HEAD
        D_FF = 1024
        NUM_STEPS = 100.0
        RESCALE = 4000.0
        EPS = 1e-05

        def _sin_emb(t):
            half = D_MODEL // 2
            x = t.astype(jnp.float32) / NUM_STEPS * RESCALE
            freqs = jnp.exp(jnp.arange(half, dtype=jnp.float32) * (-math.log(10000.0) / (half - 1)))
            e = x[:, None] * freqs[None, :]
            return jnp.concatenate([jnp.sin(e), jnp.cos(e)], axis=-1)

        def _ln(x):
            m = jnp.mean(x, axis=-1, keepdims=True)
            v = jnp.var(x, axis=-1, keepdims=True)
            return (x - m) / jnp.sqrt(v + EPS)

        def _gelu2(x):
            return x * jax.nn.sigmoid(1.702 * x)
        key = jax.random.key(seed)
        ks = jax.random.split(key, 24)
        B, S, D, F = (4, 128, D_MODEL, D_FF)
        std = 0.02
        inp = {'src': jax.random.normal(ks[0], (B, S, D), dtype=jnp.float32), 'src_mask': jax.random.randint(ks[1], (B, 1, S, S), 0, 2).astype(bool), 'timestep': jax.random.randint(ks[2], (B,), 0, 100, dtype=jnp.int32), 'attention_bias': jax.random.normal(ks[3], (B, N_HEAD, S, S), dtype=jnp.float32), 'W_ada': jax.random.normal(ks[4], (D, 2 * D), dtype=jnp.float32) * std, 'b_ada': jnp.zeros((2 * D,), dtype=jnp.float32), 'Wq': jax.random.normal(ks[5], (D, D), dtype=jnp.float32) * std, 'bq': jnp.zeros((D,), dtype=jnp.float32), 'Wk': jax.random.normal(ks[6], (D, D), dtype=jnp.float32) * std, 'bk': jnp.zeros((D,), dtype=jnp.float32), 'Wv': jax.random.normal(ks[7], (D, D), dtype=jnp.float32) * std, 'bv': jnp.zeros((D,), dtype=jnp.float32), 'Wo': jax.random.normal(ks[8], (D, D), dtype=jnp.float32) * std, 'bo': jnp.zeros((D,), dtype=jnp.float32), 'W1': jax.random.normal(ks[9], (D, F), dtype=jnp.float32) * std, 'b1': jnp.zeros((F,), dtype=jnp.float32), 'W2': jax.random.normal(ks[10], (F, D), dtype=jnp.float32) * std, 'b2': jnp.zeros((D,), dtype=jnp.float32), 'g2': jnp.ones((D,), dtype=jnp.float32), 'beta2': jnp.zeros((D,), dtype=jnp.float32)}
        return inp
    _L1_cond_all = _L1_cond_setup()
    _L1_cond_in = {k: v for k, v in _L1_cond_all.items() if k in ('W_ada', 'b_ada', 'Wq', 'bq', 'Wk', 'bk', 'Wv', 'bv', 'Wo', 'bo', 'W1', 'b1', 'W2', 'b2', 'g2', 'beta2')}
    del _L1_cond_all
    return {'x': x, 'itok_B_0_15': itok_B_0_15, 'itok_B_34_63': itok_B_34_63, 'fside_Bx16xSxS_0': fside_Bx16xSxS_0, 'mask_Bx1xSxS_bk0': mask_Bx1xSxS_bk0, 'L0_cond_down_W': _L0_cond_in['down_W'], 'L0_cond_down_b': _L0_cond_in['down_b'], 'L0_cond_up_W': _L0_cond_in['up_W'], 'L0_cond_up_b': _L0_cond_in['up_b'], 'L0_cond_expert_W': _L0_cond_in['expert_W'], 'L0_cond_expert_b': _L0_cond_in['expert_b'], 'L0_cond_domain_emb': _L0_cond_in['domain_emb'], 'L0_cond_ln_gamma': _L0_cond_in['ln_gamma'], 'L0_cond_ln_beta': _L0_cond_in['ln_beta'], 'L1_cond_W_ada': _L1_cond_in['W_ada'], 'L1_cond_b_ada': _L1_cond_in['b_ada'], 'L1_cond_Wq': _L1_cond_in['Wq'], 'L1_cond_bq': _L1_cond_in['bq'], 'L1_cond_Wk': _L1_cond_in['Wk'], 'L1_cond_bk': _L1_cond_in['bk'], 'L1_cond_Wv': _L1_cond_in['Wv'], 'L1_cond_bv': _L1_cond_in['bv'], 'L1_cond_Wo': _L1_cond_in['Wo'], 'L1_cond_bo': _L1_cond_in['bo'], 'L1_cond_W1': _L1_cond_in['W1'], 'L1_cond_b1': _L1_cond_in['b1'], 'L1_cond_W2': _L1_cond_in['W2'], 'L1_cond_b2': _L1_cond_in['b2'], 'L1_cond_g2': _L1_cond_in['g2'], 'L1_cond_beta2': _L1_cond_in['beta2']}

def reference(x, itok_B_0_15, itok_B_34_63, fside_Bx16xSxS_0, mask_Bx1xSxS_bk0, L0_cond_down_W, L0_cond_down_b, L0_cond_up_W, L0_cond_up_b, L0_cond_expert_W, L0_cond_expert_b, L0_cond_domain_emb, L0_cond_ln_gamma, L0_cond_ln_beta, L1_cond_W_ada, L1_cond_b_ada, L1_cond_Wq, L1_cond_bq, L1_cond_Wk, L1_cond_bk, L1_cond_Wv, L1_cond_bv, L1_cond_Wo, L1_cond_bo, L1_cond_W1, L1_cond_b1, L1_cond_W2, L1_cond_b2, L1_cond_g2, L1_cond_beta2):
    import jax
    import jax.numpy as jnp

    def _L0_cond_ref(hidden_states, domain_id, down_W, down_b, up_W, up_b, expert_W, expert_b, domain_emb, ln_gamma, ln_beta):
        import jax, jax.numpy as jnp
        import numpy as np
        B, S, D = (32, 256, 256)
        A = 64
        E = 16
        LN_EPS = 1e-05
        residual = hidden_states
        hidden = jnp.einsum('bsd,ad->bsa', hidden_states, down_W) + down_b
        hidden = jax.nn.gelu(hidden, approximate=False)
        valid = (domain_id >= 0) & (domain_id < E)
        idx = jnp.clip(domain_id, 0, E - 1)
        Wsel = expert_W[idx]
        bsel = expert_b[idx]
        expert_out = jnp.einsum('bsa,boa->bso', hidden, Wsel) + bsel[:, None, :]
        domain_output = jnp.where(valid[:, None, None], expert_out, hidden)
        hidden = domain_output + domain_emb[idx][:, None, :]
        hidden = jnp.einsum('bsa,da->bsd', hidden, up_W) + up_b
        x = hidden + residual
        mu = jnp.mean(x, axis=-1, keepdims=True)
        var = jnp.mean(jnp.square(x - mu), axis=-1, keepdims=True)
        return (x - mu) * jax.lax.rsqrt(var + LN_EPS) * ln_gamma + ln_beta

    def _L1_cond_ref(src, src_mask, timestep, attention_bias, W_ada, b_ada, Wq, bq, Wk, bk, Wv, bv, Wo, bo, W1, b1, W2, b2, g2, beta2):
        import jax, jax.numpy as jnp
        import numpy as np
        import math
        D_MODEL = 256
        N_HEAD = 16
        HEAD_DIM = D_MODEL // N_HEAD
        D_FF = 1024
        NUM_STEPS = 100.0
        RESCALE = 4000.0
        EPS = 1e-05

        def _sin_emb(t):
            half = D_MODEL // 2
            x = t.astype(jnp.float32) / NUM_STEPS * RESCALE
            freqs = jnp.exp(jnp.arange(half, dtype=jnp.float32) * (-math.log(10000.0) / (half - 1)))
            e = x[:, None] * freqs[None, :]
            return jnp.concatenate([jnp.sin(e), jnp.cos(e)], axis=-1)

        def _ln(x):
            m = jnp.mean(x, axis=-1, keepdims=True)
            v = jnp.var(x, axis=-1, keepdims=True)
            return (x - m) / jnp.sqrt(v + EPS)

        def _gelu2(x):
            return x * jax.nn.sigmoid(1.702 * x)
        B, S, D = src.shape
        emb = jax.nn.silu(_sin_emb(timestep)) @ W_ada + b_ada
        scale, shift = jnp.split(emb[:, None, :], 2, axis=-1)
        x = _ln(src) * (1.0 + scale) + shift
        q = (x @ Wq + bq).reshape(B, S, N_HEAD, HEAD_DIM).transpose(0, 2, 1, 3)
        k = (x @ Wk + bk).reshape(B, S, N_HEAD, HEAD_DIM).transpose(0, 2, 1, 3)
        v = (x @ Wv + bv).reshape(B, S, N_HEAD, HEAD_DIM).transpose(0, 2, 1, 3)
        scores = jnp.einsum('bhqd,bhkd->bhqk', q / math.sqrt(HEAD_DIM), k)
        scores = scores + attention_bias
        scores = jnp.where(src_mask, -jnp.inf, scores.astype(jnp.float32))
        probs = jax.nn.softmax(scores, axis=-1).astype(v.dtype)
        ctx = jnp.einsum('bhqk,bhkd->bhqd', probs, v)
        ctx = ctx.transpose(0, 2, 1, 3).reshape(B, S, D)
        x = x + (ctx @ Wo + bo)
        h = _ln(x) * g2 + beta2
        ff = _gelu2(h @ W1 + b1) @ W2 + b2
        return x + ff
    x = _L0_cond_ref(x, itok_B_0_15, L0_cond_down_W, L0_cond_down_b, L0_cond_up_W, L0_cond_up_b, L0_cond_expert_W, L0_cond_expert_b, L0_cond_domain_emb, L0_cond_ln_gamma, L0_cond_ln_beta)
    x = _L1_cond_ref(x, mask_Bx1xSxS_bk0, itok_B_34_63, fside_Bx16xSxS_0, L1_cond_W_ada, L1_cond_b_ada, L1_cond_Wq, L1_cond_bq, L1_cond_Wk, L1_cond_bk, L1_cond_Wv, L1_cond_bv, L1_cond_Wo, L1_cond_bo, L1_cond_W1, L1_cond_b1, L1_cond_W2, L1_cond_b2, L1_cond_g2, L1_cond_beta2)
    return x

_drawn_inputs = setup_inputs


def setup_inputs(seed=0):
    import zlib

    import numpy as np

    out = dict(_drawn_inputs(seed))
    spreads = {'L0_cond_ln_gamma': (1.0, 0.2),
     'L0_cond_ln_beta': (0.0, 0.1),
     'L1_cond_b_ada': (0.0, 0.1),
     'L1_cond_bq': (0.0, 0.8),
     'L1_cond_bk': (0.0, 0.8),
     'L1_cond_bv': (0.0, 0.268),
     'L1_cond_bo': (0.0, 0.1),
     'L1_cond_b1': (0.0, 0.1),
     'L1_cond_b2': (0.0, 0.1),
     'L1_cond_g2': (1.0, 0.6),
     'L1_cond_beta2': (0.0, 0.684)}
    factors = {'fside_Bx16xSxS_0': 8.0, 'L0_cond_down_b': 8.0, 'L1_cond_Wq': 8.0, 'L1_cond_Wk': 8.0}
    for name, (base, spread) in spreads.items():
        noise = np.random.default_rng([zlib.crc32(name.encode()), seed]).standard_normal(out[name].shape)
        drawn = base * np.exp(spread * noise) if base else spread * noise
        out[name] = jnp.asarray(drawn.astype(out[name].dtype))
    for name, factor in factors.items():
        out[name] = (out[name] * factor).astype(out[name].dtype)
    return out
```

```python
from contextlib import ExitStack

import numpy as np

import concourse.bass as bass
from concourse import mybir

F32 = mybir.dt.float32
BF16 = mybir.dt.bfloat16
I32 = mybir.dt.int32
U8 = mybir.dt.uint8
ALU = mybir.AluOpType
ACT = mybir.ActivationFunctionType

P = 128
B, S, D = 8, 512, 256
H, HD = 16, 16
A, E = 64, 16
F = 1024
EPS = 1e-5
CH = 256
NCH = B * S // CH
CT = D // P
FT = F // P
GH = 4
TI = 32
KT = S // P
LAG_T = 3
LAG_C = 4
MASKED = 1e30
BIG = 3.0e38
K_SLOTS = 5
RUNS = [(0, 3, 1), (48, 3, 2), (96, 2, 0)]
GATE = 1.702 / 2
FIRST, LAST = -2, NCH + 2
PRE_CHAIN, MID_CHAIN, FFN_CHAIN = 8, 1, 4
VEC = {"bq": 0, "bk": 2, "g2": 4, "beta2": 6, "b1": 8, "down_b": 16, "freq": 17}
TWO_PI = 2 * np.pi
C1 = 6.28125
C2 = float(np.round((TWO_PI - C1) * 2**21) / 2**21)
C3 = float(TWO_PI - C1 - C2)
MAGIC = 1.5 * 2.0**23
PI_IN = 3.1415925


def stages(i):
    return 0 <= i < NCH, 1 <= i <= NCH, i + 2 < NCH, 0 <= i - 2 < NCH, 0 <= i - 3 < NCH


def wait(eng, sem, value):
    if isinstance(value, int) and value <= 0:
        return
    eng.wait_ge(sem, value)


def apart(eng):
    eng.nop(nofuse=True)


def each_iteration(eng, body):
    for i in range(FIRST, 3):
        body(i, *stages(i))
    with eng.Fori(3, NCH - 2) as i:
        body(i, *stages(3))
    for i in range(NCH - 2, LAST + 1):
        body(i, *stages(i))


def build(nc, x, t_tok, e_tok, bias, mask, downT, upT, up_b, expertT, expert_be, gamma, beta,
          w_ada, b_ada, wq, wk, wv, bv, wo, bo, w1, w2, b2, vecs, ident_in, out):
    x_v = x.rearrange("(c j p) d -> c p j d", j=2, p=P)
    out_v = out.rearrange("(c j p) d -> c p j d", j=2, p=P)
    bias_v = bias.rearrange("h (q p) k -> h p q k", p=P)
    mask_v = mask.rearrange("b (q p) k -> b p q k", p=P)

    def dram(name, shape, dt):
        return nc.dram_tensor(name, shape, dt, kind="Internal").ap()

    q_d = dram("q_parts", (B, H, 3 * HD, S), BF16)
    k_d = dram("k_parts", (B, H, K_SLOTS * HD, S), BF16)
    v_d = dram("v_rows", (B * S, D), F32)
    xs_d = dram("x_rows", (B * S, D), F32)
    ctx_d = dram("ctx_rows", (B * S, D), F32)
    emb_d = dram("emb_rows", (B, 2 * D), F32)
    ew_d = dram("expert_rows", (B, A, A + 1), F32)
    xs_v = xs_d.rearrange("(c j p) d -> c p j d", j=2, p=P)
    ctx_v = ctx_d.rearrange("(c j p) d -> c p j d", j=2, p=P)
    v_v = v_d.rearrange("(c j p) d -> c p j d", j=2, p=P)
    v_b = v_d.rearrange("(b k p) d -> b p k d", k=KT, p=P)
    ctx_b = ctx_d.rearrange("(b k p) d -> b p k d", k=KT, p=P)

    with ExitStack() as ctx:
        def sb(name, shape, dt=F32):
            return ctx.enter_context(nc.sbuf_tensor(name, shape, dt))

        def ps(name):
            return ctx.enter_context(nc.psum_tensor(name, [P, 512], F32))

        def sem(name):
            return ctx.enter_context(nc.semaphore(name))

        ident = sb("ident", [P, P])
        down_w = sb("down_w", [P, CT, A])
        up_w = sb("up_w", [P, D])
        wq_s = sb("wq_s", [P, CT, D])
        wk_s = sb("wk_s", [P, CT, D])
        wv_s = sb("wv_s", [P, CT, D])
        wo_s = sb("wo_s", [P, CT, D])
        w1_s = sb("w1_s", [P, CT, F])
        w2_s = sb("w2_s", [P, FT, D])
        gamma_r = sb("gamma_r", [P, D])
        beta_r = sb("beta_r", [P, D])
        bo_r = sb("bo_r", [P, D])
        bv_r = sb("bv_r", [P, D])
        b2_r = sb("b2_r", [P, D])
        vec = sb("vec", [P, 18])
        nbq = sb("nbq", [P, 2])
        b1g = sb("b1g", [P, FT])
        powc = sb("powc", [P, 2])

        bias_s = sb("bias_s", [P, GH, KT, S])
        mask_raw = sb("mask_raw", [P, KT, S], U8)
        mask_f = sb("mask_f", [P, KT, S])
        stq = [sb(f"stq{g}", [P, GH, S], BF16) for g in range(2)]
        stk = [sb(f"stk{g}", [P, GH, S], BF16) for g in range(2)]
        v_s = [sb(f"v_s{g}", [P, KT, GH * HD + HD]) for g in range(2)]
        pT = [sb(f"pT{g}", [P, GH, KT, S]) for g in range(2)]
        mx = sb("mx", [P, TI])
        sums = sb("sums", [P, TI])
        rinv = sb("rinv", [P, 16])
        cT = sb("cT", [P, S])
        cn = [sb(f"cn{g}", [P, KT, GH * HD]) for g in range(2)]

        xin = sb("xin", [P, 2, D])
        xT = sb("xT", [P, CT, CH])
        g_s = sb("g_s", [P, CH])
        h2 = sb("h2", [P, CH])
        ewx = sb("ewx", [P, A + 1])
        mod = sb("mod", [P, 2 * D])
        xm = sb("xm", [P, 2, D])
        xs = sb("xs", [P, 2, D])
        qk = sb("qk", [P, 4 * CH])
        qkb = sb("qkb", [P, 3, 4 * CH], BF16)
        vs = sb("vs", [P, 2, D])
        st = sb("st", [P, 2, 6])
        mv0 = sb("mv0", [P, 2, 2])
        mv1 = sb("mv1", [P, 2, 2])
        rs0 = sb("rs0", [P, 2])
        rs1 = sb("rs1", [P, 2])

        cin = sb("cin", [P, 2, D])
        xsin = sb("xsin", [P, 2, D])
        cT2 = sb("cT2", [P, CT, CH])
        x2 = sb("x2", [P, 2, D])
        x2b = sb("x2b", [P, 2, D])
        hT = sb("hT", [P, CT, CH])
        st2 = sb("st2", [P, 2, 6])
        mv2 = sb("mv2", [P, 2, 2])
        rs2 = sb("rs2", [P, 2])
        th = sb("th", [P, 2 * CH])
        act_s = sb("act_s", [P, FT, CH])

        t_i = sb("t_i", [P, B], I32)
        e_i = sb("e_i", [P, B], I32)
        idx_i = sb("idx_i", [P, B], I32)
        sm = sb("sm", [P, 16, 2 * B])
        tb = sb("tb", [P, B], BF16)
        w_ada_s = pT[0][:, 0, 0:2, :]
        ew_all = pT[0][0:A, 1, 0:1, :].rearrange("p a (b o) -> p (a b) o", b=B)
        ew_fin = pT[0][0:A, 2, 0:2, :].rearrange("p a n -> p (a n)")[:, 0:B * (A + 1)].rearrange(
            "p (b o) -> p b o", b=B)
        ebe = pT[0][0:A, 3, 0, 0:2 * B].rearrange("p (b o) -> p b o", b=B)
        ada_r = pT[0][0:B, 1, 1, :]
        emb_s = pT[0][0:B, 1, 2, :]

        sc = [ps("sc0"), ps("sc1")]
        tp = [ps("tp0"), ps("tp1")]
        pv = ps("pv")
        la, lb, lc = ps("la"), ps("lb"), ps("lc")

        names = """setup_in up_zero u_zero setup_chain setup_dve setup_act setup_pe idx_ready expert_in setup_store
            mask_in mask_ready masked sc_ready smax probs pt_ready copied_v copied_a pv_done ctxT_ready
            ctxn_tr ctx_norm dve_rinv x_in p_xt a_xt p_down a_gelu p_exp a_h2 p_up d_x1 d_mv0 g_rs0
            d_mv1 g_rs1 d_xm p_xt1 a_xt1 p_q p_k a_q a_k d_split p_v d_v g_xs xs_out qkv_out pre_chain
            pool_pre cx_in p_ct a_ct p_wo d_x2 d_mv2 g_rs2 g_x2b d_hn p_ht a_hT mid_chain pool_mid
            p_w1 a_th d_act p_w2 d_out ffn_chain out_out""".split()
        s = {n: sem(n) for n in names}
        bias_in = [sem(f"bias_in{n}") for n in range(GH)]
        stack_in = [sem(f"stack_in{g}") for g in range(2)]
        v_in = [sem(f"v_in{g}") for g in range(2)]
        ctx_out = [sem(f"ctx_out{g}") for g in range(2)]
        SETUP_LOADS = 20
        STACK_LOADS = 6
        QKV_STORES = 3 + K_SLOTS + 1

        block = ctx.enter_context(nc.Block())

        @block.sync
        def _(sp):
            def wait(eng, sem, value):
                if isinstance(value, int) and value <= 0:
                    return
                eng.wait_ge(sem, value)
                if not isinstance(value, int):
                    apart(eng)

            def load_bias(i, hh):
                wait(sp, s["pt_ready"], TI * i + 4 * hh - 12)
                sp.dma_start(bias_s[:, hh % GH, :, :],
                             bias_v[bass.ds(8 * i + hh, 1)].rearrange("h p q k -> (h p) q k")
                             ).then_inc(bias_in[hh % GH], 16)

            def load_mask(i):
                wait(sp, s["mask_ready"], i)
                sp.dma_start(mask_raw[:, :, :],
                             mask_v[bass.ds(i // 2, 1)].rearrange("b p q k -> (b p) q k")
                             ).then_inc(s["mask_in"], 16)

            def load_stack(i, g):
                head = (i % 2) * 8 + GH * g
                wait(sp, s["sc_ready"], TI * (i - 1) + 16 * (g + 1))
                for row, parts, k0 in RUNS:
                    n = parts * HD
                    qsrc = q_d[bass.ds(i // 2, 1), bass.ds(head, GH), 0:n, :]
                    ksrc = k_d[bass.ds(i // 2, 1), bass.ds(head, GH), k0 * HD:k0 * HD + n, :]
                    sp.dma_start(stq[g][row:row + n], qsrc.rearrange("b h r t -> (b r) h t")
                                 ).then_inc(stack_in[g], 16)
                    sp.dma_start(stk[g][row:row + n], ksrc.rearrange("b h r t -> (b r) h t")
                                 ).then_inc(stack_in[g], 16)

            def load_v(i, g):
                wait(sp, s["pv_done"], 2 * (i - 1) + g + 1)
                col = ((i % 2) * 8 + GH * g) * HD
                sp.dma_start(v_s[g][:, :, 0:GH * HD],
                             v_b[bass.ds(i // 2, 1), :, :, bass.ds(col, GH * HD)].rearrange(
                                 "b p k d -> (b p) k d")).then_inc(v_in[g], 16)

            def store_ctx(i, g):
                wait(sp, s["ctx_norm"], 2 * i + g + 1)
                col = ((i % 2) * 8 + GH * g) * HD
                sp.dma_start(ctx_b[bass.ds(i // 2, 1), :, :, bass.ds(col, GH * HD)].rearrange(
                    "b p k d -> (b p) k d"), cn[g][:, :, :]).then_inc(ctx_out[g], 16)

            def rows(view, c):
                return view[bass.ds(c, 1)].rearrange("c p j d -> (c p) j d")

            loads = [(ident[:, :], ident_in), (down_w[:, :, :], downT.rearrange("(c p) a -> p c a", p=P)),
                     (up_w[0:A, :], upT), (wq_s[:, :, :], wq.rearrange("(c p) n -> p c n", p=P)),
                     (wk_s[:, :, :], wk.rearrange("(c p) n -> p c n", p=P)),
                     (wv_s[:, :, :], wv.rearrange("(c p) n -> p c n", p=P)),
                     (wo_s[:, :, :], wo.rearrange("(c p) n -> p c n", p=P)),
                     (w1_s[:, :, :], w1.rearrange("(c p) n -> p c n", p=P)),
                     (w2_s[:, :, :], w2.rearrange("(c p) n -> p c n", p=P)),
                     (w_ada_s, w_ada.rearrange("(c p) n -> p c n", p=P)),
                     (gamma_r[:, :], gamma.to_broadcast([P, D])), (beta_r[:, :], beta.to_broadcast([P, D])),
                     (bo_r[:, :], bo.to_broadcast([P, D])), (bv_r[:, :], bv.to_broadcast([P, D])),
                     (b2_r[:, :], b2.to_broadcast([P, D])), (vec[:, :], vecs),
                     (ada_r, b_ada.to_broadcast([B, 2 * D])),
                     (t_i[:, :], t_tok.to_broadcast([P, B])), (e_i[:, :], e_tok.to_broadcast([P, B]))]
            for dst, src in loads:
                sp.dma_start(dst, src).then_inc(s["setup_in"], 16)
            sp.wait_ge(s["up_zero"], 1)
            sp.dma_start(up_w[A:A + 1, :], up_b).then_inc(s["setup_in"], 16)
            for hh in range(3):
                load_bias(0, hh)
            load_mask(0)
            sp.wait_ge(s["idx_ready"], 1)
            sp.wait_ge(s["setup_in"], 16 * SETUP_LOADS)
            for b in range(B):
                e = sp.value_load(idx_i[0:1, b:b + 1], min_val=0, max_val=E - 1)
                sp.dma_start(ew_all[:, b, :], expertT[bass.ds(e, 1)].rearrange("e a o -> (e a) o")
                             ).then_inc(s["expert_in"], 16)
                sp.dma_start(ebe[:, b, :], expert_be[bass.ds(e, 1)].rearrange("e a o -> (e a) o")
                             ).then_inc(s["expert_in"], 16)
            sp.wait_ge(s["setup_dve"], 1)
            sp.dma_start(ew_d.rearrange("b a o -> a b o"), ew_fin).then_inc(s["setup_store"], 16)
            sp.wait_ge(s["setup_dve"], 2)
            sp.dma_start(emb_d, emb_s).then_inc(s["setup_store"], 16)
            sp.wait_ge(s["setup_store"], 32)

            def body(i, attn, prev, pre, mid, ffn):
                c = i + 2
                if attn and not (isinstance(i, int) and i == 0):
                    load_mask(i)
                    load_bias(i, 0)
                if pre:
                    wait(sp, s["d_xm"], c)
                    sp.dma_start(xin[:, :, :], rows(x_v, c)).then_inc(s["x_in"], 16)
                    wait(sp, s["p_exp"], c)
                    wait(sp, s["a_h2"], c)
                    sp.dma_start(ewx[0:A, :], ew_d[bass.ds(c // 2, 1)].rearrange("b a o -> (b a) o")
                                 ).then_inc(s["x_in"], 16)
                    sp.dma_start(mod[:, :], emb_d[bass.ds(c // 2, 1)].to_broadcast([P, 2 * D])
                                 ).then_inc(s["x_in"], 16)
                if prev:
                    store_ctx(i - 1, 0)
                if attn:
                    n_stored = i + 2 if pre else NCH
                    wait(sp, s["qkv_out"], 16 * QKV_STORES * n_stored)
                    load_stack(i, 0)
                    load_v(i, 0)
                    if not (isinstance(i, int) and i == 0):
                        load_bias(i, 1)
                        load_bias(i, 2)
                    load_stack(i, 1)
                    load_bias(i, 3)
                    load_v(i, 1)
                    load_bias(i, 4)
                if prev:
                    store_ctx(i - 1, 1)
                if attn:
                    load_bias(i, 5)
                if mid:
                    m = i - 2
                    for g in range(2):
                        wait(sp, ctx_out[g], 16 * i if prev else 16 * NCH)
                    wait(sp, s["xs_out"], 16 * (i + 2) if pre else 16 * NCH)
                    wait(sp, s["p_ct"], m)
                    wait(sp, s["p_ht"], m)
                    sp.dma_start(cin[:, :, :], rows(ctx_v, m)).then_inc(s["cx_in"], 16)
                    sp.dma_start(xsin[:, :, :], rows(xs_v, m)).then_inc(s["cx_in"], 16)
                if pre:
                    wait(sp, s["g_xs"], c + 1)
                    sp.dma_start(rows(xs_v, c), xs[:, :, :]).then_inc(s["xs_out"], 16)
                if attn:
                    load_bias(i, 6)
                if pre:
                    wait(sp, s["d_v"], c + 1)
                    sp.dma_start(rows(v_v, c), vs[:, :, :]).then_inc(s["qkv_out"], 16)
                    wait(sp, s["d_split"], c + 1)
                    parts = [(q_d, n, n, 0) for n in range(3)] + [(k_d, n, n % 3, 2 * CH) for n in range(K_SLOTS)]
                    for dst, slot, part, off in parts:
                        sp.dma_start(
                            dst[bass.ds(c // 2, 1), :, slot * HD:(slot + 1) * HD,
                                bass.ds((c % 2) * CH, CH)].rearrange("b h d t -> (b d) h t"),
                            qkb[:, part, off:off + 2 * CH].rearrange("p (m t) -> p m t", m=2)
                        ).then_inc(s["qkv_out"], 16)
                if attn:
                    load_bias(i, 7)
                if ffn:
                    wait(sp, s["d_out"], i - 3 + 1)
                    sp.dma_start(rows(out_v, i - 3), x2b[:, :, :]).then_inc(s["out_out"], 16)

            each_iteration(sp, body)
            sp.wait_ge(s["out_out"], 16 * NCH)
            sp.wait_ge(s["xs_out"], 16 * NCH)
            sp.wait_ge(s["qkv_out"], 16 * QKV_STORES * NCH)
            for g in range(2):
                sp.wait_ge(ctx_out[g], 16 * NCH)

        @block.gpsimd
        def _(pool):
            pool.memset(powc[:, :], -0.5).then_inc(s["pool_pre"], 1)
            pool.memset(v_s[0][:, :, :], 0.0).then_inc(s["u_zero"], 1)
            pool.memset(v_s[1][:, :, :], 0.0).then_inc(s["u_zero"], 1)
            pool.wait_ge(s["pool_pre"], 1)
            pool.wait_ge(s["setup_in"], 16 * SETUP_LOADS)

            def mask_head(i, hh):
                pool.wait_ge(bias_in[hh % GH], 16 * (2 * i + hh // GH + 1))
                for half in range(2):
                    b = bias_s[:, hh % GH, 2 * half:2 * half + 2, :]
                    pool.tensor_tensor(b, mask_f[:, 2 * half:2 * half + 2, :], b, ALU.subtract
                                       ).then_inc(s["masked"], 1)

            def rsqrt(chain, base, var, dst):
                apart(pool)
                pool.tensor_scalar(dst, var, EPS, 1.0, ALU.add, ALU.mult).then_inc(s[chain], 1)
                pool.wait_ge(s[chain], base)
                return pool.tensor_tensor(dst, dst, powc[:, :], ALU.pow)

            def body(i, attn, prev, pre, mid, ffn):
                c, m = i + 2, i - 2
                if attn:
                    pool.wait_ge(s["mask_in"], 16 * (i + 1))
                    wait(pool, s["masked"], 16 * i)
                    apart(pool)
                    pool.tensor_scalar(mask_f[:, :, :], mask_raw[:, :, :], MASKED, 0.0, ALU.mult, ALU.add
                                       ).then_inc(s["mask_ready"], 1)
                    pool.wait_ge(s["mask_ready"], i + 1)
                    for hh in range(4):
                        mask_head(i, hh)
                if pre:
                    pool.wait_ge(s["d_mv0"], c + 1)
                    wait(pool, s["d_mv1"], c)
                    rsqrt("pool_pre", 2 * c + 2, mv0[:, :, 1], rs0[:, :]).then_inc(s["g_rs0"], 1)
                    pool.wait_ge(s["d_mv1"], c + 1)
                    wait(pool, s["d_xm"], c)
                    rsqrt("pool_pre", 2 * c + 3, mv1[:, :, 1], rs1[:, :]).then_inc(s["g_rs1"], 1)
                if attn:
                    mask_head(i, 4)
                if pre:
                    pool.wait_ge(s["d_xm"], c + 1)
                    wait(pool, s["xs_out"], 16 * c)
                    pool.tensor_tensor(xs[:, :, :], xm[:, :, :],
                                       bo_r[:, :].unsqueeze(1).to_broadcast([P, 2, D]), ALU.add
                                       ).then_inc(s["g_xs"], 1)
                if attn:
                    for hh in range(5, 8):
                        mask_head(i, hh)
                if mid:
                    pool.wait_ge(s["d_mv2"], m + 1)
                    wait(pool, s["d_hn"], m)
                    rsqrt("pool_mid", m + 1, mv2[:, :, 1], rs2[:, :]).then_inc(s["g_rs2"], 1)
                    wait(pool, s["out_out"], 16 * m)
                    pool.tensor_tensor(x2b[:, :, :], x2[:, :, :],
                                       b2_r[:, :].unsqueeze(1).to_broadcast([P, 2, D]), ALU.add
                                       ).then_inc(s["g_x2b"], 1)

            each_iteration(pool, body)

        @block.tensor
        def _(pe):
            def transposes(dst, src, done):
                for ct in range(CT):
                    for j in range(2):
                        last = pe.transpose(dst[:, ct * CH + j * P:ct * CH + (j + 1) * P],
                                            src[:, j, ct * P:(ct + 1) * P], ident[:, :])
                last.then_inc(s[done], 1)

            pe.wait_ge(s["setup_in"], 16 * SETUP_LOADS)
            pe.wait_ge(s["setup_dve"], 1)
            for j in range(2):
                last = pe.matmul(lc[0:B, :], sm[:, 15, j * B:(j + 1) * B], w_ada_s[:, j, :],
                                 start=(j == 0), stop=(j == 1))
            last.then_inc(s["setup_pe"], 1)
            pe.wait_ge(s["setup_dve"], 2)
            pe.wait_ge(s["u_zero"], 5)

            def body(i, attn, prev, pre, mid, ffn):
                c, m, f = i + 2, i - 2, i - 3
                for t in range(TI):
                    if attn:
                        hh, qt = t // 4, t % 4
                        g = hh // GH
                        if t % 16 == 0:
                            pe.wait_ge(stack_in[g], 16 * STACK_LOADS * (i + 1))
                        wait(pe, s["smax"], TI * i + t - 1)
                        pe.matmul(sc[t % 2][:, :], stq[g][:, hh % GH, qt * P:(qt + 1) * P],
                                  stk[g][:, hh % GH, :], start=True, stop=True).then_inc(s["sc_ready"], 1)

                    if pre and t == 0:
                        pe.wait_ge(s["x_in"], 48 * (c + 1))
                        wait(pe, s["a_hT"], m)
                        transposes(la, xin, "p_xt")
                    if pre and t == 2:
                        pe.wait_ge(s["a_xt"], c + 1)
                        wait(pe, s["d_x2"], m)
                        for ct in range(CT):
                            last = pe.matmul(lb[0:A, 0:CH], down_w[:, ct, :], xT[:, ct, :],
                                             start=(ct == 0), stop=(ct == CT - 1))
                        last.then_inc(s["p_down"], 1)
                    if pre and t == 4:
                        pe.wait_ge(s["a_gelu"], c + 1)
                        pe.matmul(la[0:A, 0:CH], ewx[:, 0:A], g_s[:, :], start=True, stop=True
                                  ).then_inc(s["p_exp"], 1)
                    if pre and t == 6:
                        pe.wait_ge(s["a_h2"], c + 1)
                        for j in range(2):
                            last = pe.matmul(lb[:, j * D:(j + 1) * D], h2[:, j * P:(j + 1) * P], up_w[:, :],
                                             start=True, stop=True)
                        last.then_inc(s["p_up"], 1)
                    if pre and t == 12:
                        pe.wait_ge(s["d_xm"], c + 1)
                        transposes(la, xm, "p_xt1")
                    if pre and t in (14, 15):
                        w, dst, done = ((wq_s, lb, "p_q"), (wk_s, la, "p_k"))[t - 14]
                        pe.wait_ge(s["a_xt1"], c + 1)
                        for mt in range(2):
                            for ct in range(CT):
                                last = pe.matmul(dst[:, mt * CH:(mt + 1) * CH], w[:, ct, mt * P:(mt + 1) * P],
                                                 xT[:, ct, :], start=(ct == 0), stop=(ct == CT - 1))
                        last.then_inc(s[done], 1)
                    if pre and t == 17:
                        pe.wait_ge(s["a_q"], c + 1)
                        for j in range(2):
                            for ct in range(CT):
                                last = pe.matmul(lb[:, j * D:(j + 1) * D], xT[:, ct, j * P:(j + 1) * P],
                                                 wv_s[:, ct, :], start=(ct == 0), stop=(ct == CT - 1))
                        last.then_inc(s["p_v"], 1)

                    if ffn and t in (1, 4, 7, 10):
                        p = t // 3
                        pe.wait_ge(s["a_hT"], f + 1)
                        if p == 0:
                            wait(pe, s["d_out"], f)
                        else:
                            pe.wait_ge(s["d_act"], 4 * f + p)
                        for n in range(2):
                            ft = 2 * p + n
                            for ct in range(CT):
                                last = pe.matmul(lc[:, n * CH:(n + 1) * CH], w1_s[:, ct, ft * P:(ft + 1) * P],
                                                 hT[:, ct, :], start=(ct == 0), stop=(ct == CT - 1))
                        last.then_inc(s["p_w1"], 1)
                    if ffn and t in (12, 14, 16, 18):
                        r = (t - 12) // 2
                        j = r // 2
                        pe.wait_ge(s["d_act"], 4 * f + 4)
                        for ft in range(4 * (r % 2), 4 * (r % 2) + 4):
                            last = pe.matmul(lc[:, j * D:(j + 1) * D], act_s[:, ft, j * P:(j + 1) * P],
                                             w2_s[:, ft, :], start=(ft == 0), stop=(ft == FT - 1))
                        last.then_inc(s["p_w2"], 1)

                    if mid and t == 19:
                        pe.wait_ge(s["cx_in"], 32 * (m + 1))
                        if pre:
                            pe.wait_ge(s["a_k"], c + 1)
                        else:
                            wait(pe, s["a_hT"], m)
                        transposes(la, cin, "p_ct")
                    if mid and t == 21:
                        pe.wait_ge(s["a_ct"], m + 1)
                        if pre:
                            pe.wait_ge(s["d_v"], c + 1)
                        else:
                            wait(pe, s["d_x2"], m)
                        for j in range(2):
                            for ct in range(CT):
                                last = pe.matmul(lb[:, j * D:(j + 1) * D], cT2[:, ct, j * P:(j + 1) * P],
                                                 wo_s[:, ct, :], start=(ct == 0), stop=(ct == CT - 1))
                        last.then_inc(s["p_wo"], 1)
                    if mid and t == 26:
                        pe.wait_ge(s["d_hn"], m + 1)
                        transposes(la, xsin, "p_ht")

                    u = t - LAG_T
                    if attn if u >= 0 else prev:
                        pe.wait_ge(s["probs"], TI * i + u + 1)
                        wait(pe, s["copied_a" if u % 2 else "copied_v"], 16 * i + u // 2)
                        src = bias_s[:, (u // 4) % GH, u % 4, :]
                        for kt in range(KT):
                            last = pe.transpose(tp[u % 2][:, kt * P:(kt + 1) * P],
                                                src[:, kt * P:(kt + 1) * P], ident[:, :])
                        last.then_inc(s["pt_ready"], 1)

                    g = 0 if t >= 16 else 1
                    gi = 2 * i + g if g == 0 else 2 * i - 1
                    if (attn if g == 0 else prev) and t % 16 in (4, 5, 6, 7):
                        kt = t % 4
                        if kt == 0:
                            pe.wait_ge(s["copied_v"], 8 * (gi + 1))
                            pe.wait_ge(s["copied_a"], 8 * (gi + 1))
                            pe.wait_ge(v_in[g], 16 * (i + 1 - g))
                            wait(pe, s["ctx_norm"], gi)
                        for h in range(GH):
                            last = pe.matmul(pv[32 * h:32 * h + 32, :], v_s[g][:, kt, HD * h:HD * h + 32],
                                             pT[g][:, h, kt, :], start=(kt == 0), stop=(kt == KT - 1),
                                             tile_position=(0, 32 * h))
                        if kt == KT - 1:
                            last.then_inc(s["pv_done"], 1)
                    if (attn if g == 0 else prev) and t % 16 == 9:
                        pe.wait_ge(s["ctxT_ready"], gi + 1)
                        for qt in range(KT):
                            last = pe.transpose(pv[:, qt * P:(qt + 1) * P], cT[:, qt * P:(qt + 1) * P],
                                                ident[:, :])
                        last.then_inc(s["ctxn_tr"], 1)

            each_iteration(pe, body)

        @block.scalar
        def _(act):
            act.wait_ge(s["idx_ready"], 2)
            act.activation(sm[:, 12, :], sm[:, 11, :], ACT.Sin).then_inc(s["setup_act"], 1)
            act.wait_ge(s["setup_act"], 1)
            act.activation(sm[:, 13, :], sm[:, 12, :], ACT.Exp, scale=-1.0).then_inc(s["setup_act"], 1)
            act.wait_ge(s["setup_in"], 16 * SETUP_LOADS)
            act.wait_ge(s["setup_dve"], 2)
            act.wait_ge(s["u_zero"], 5)

            def body(i, attn, prev, pre, mid, ffn):
                c, m, f = i + 2, i - 2, i - 3
                for t in range(TI):
                    if attn:
                        hh, qt = t // 4, t % 4
                        act.wait_ge(s["smax"], TI * i + t + 1)
                        tile = bias_s[:, hh % GH, qt, :]
                        act.activation(tile, tile, ACT.Exp, bias=mx[:, t:t + 1], scale=-1.0,
                                       accum_out=sums[:, t:t + 1]).then_inc(s["probs"], 1)

                    u = t - LAG_C
                    if (attn if u >= 0 else prev) and u % 2 == 1:
                        uu = u % TI
                        g = uu // 16
                        act.wait_ge(s["pt_ready"], TI * i + u + 1)
                        if uu % 16 == 1:
                            wait(act, s["pv_done"], 2 * i + g - 1)
                        act.copy(pT[g][:, (uu // 4) % GH, :, (u % 4) * P:(u % 4 + 1) * P],
                                 tp[1][:, :].rearrange("p (k q) -> p k q", k=KT)).then_inc(s["copied_a"], 1)

                    if (attn if t >= 16 else prev) and t % 16 == 8:
                        gi = 2 * i if t >= 16 else 2 * i - 1
                        act.wait_ge(s["pv_done"], gi + 1)
                        wait(act, s["ctxn_tr"], gi)
                        act.copy(cT[:, :], pv[:, :]).then_inc(s["ctxT_ready"], 1)

                    if pre and t == 1:
                        act.wait_ge(s["p_xt"], c + 1)
                        act.copy(xT[:, :, :].rearrange("p c n -> p (c n)"), la[:, :]).then_inc(s["a_xt"], 1)
                    if pre and t == 3:
                        act.wait_ge(s["p_down"], c + 1)
                        act.activation(g_s[0:A, :], lb[0:A, 0:CH], ACT.Gelu,
                                       bias=vec[0:A, VEC["down_b"]:VEC["down_b"] + 1]).then_inc(s["a_gelu"], 1)
                    if pre and t == 5:
                        act.wait_ge(s["p_exp"], c + 1)
                        act.activation(h2[0:A, :], la[0:A, 0:CH], ACT.Identity, bias=ewx[0:A, A:A + 1]
                                       ).then_inc(s["a_h2"], 1)
                    if pre and t == 13:
                        act.wait_ge(s["p_xt1"], c + 1)
                        act.copy(xT[:, :, :].rearrange("p c n -> p (c n)"), la[:, :]).then_inc(s["a_xt1"], 1)
                    if pre and t == 15:
                        act.wait_ge(s["p_q"], c + 1)
                        wait(act, s["d_split"], c)
                        for mt in range(2):
                            last = act.activation(qk[:, mt * CH:(mt + 1) * CH], lb[:, mt * CH:(mt + 1) * CH],
                                                  ACT.Identity, scale=-0.25, bias=nbq[:, mt:mt + 1])
                        last.then_inc(s["a_q"], 1)
                    if pre and t == 16:
                        act.wait_ge(s["p_k"], c + 1)
                        for mt in range(2):
                            last = act.activation(qk[:, (2 + mt) * CH:(3 + mt) * CH],
                                                  la[:, mt * CH:(mt + 1) * CH], ACT.Identity,
                                                  bias=vec[:, VEC["bk"] + mt:VEC["bk"] + mt + 1])
                        last.then_inc(s["a_k"], 1)

                    if ffn and t in (2, 5, 8, 11):
                        p = t // 3
                        act.wait_ge(s["p_w1"], 4 * f + p + 1)
                        wait(act, s["d_act"], 4 * f + p)
                        for n in range(2):
                            ft = 2 * p + n
                            last = act.activation(th[:, n * CH:(n + 1) * CH], lc[:, n * CH:(n + 1) * CH],
                                                  ACT.Tanh, scale=GATE, bias=b1g[:, ft:ft + 1])
                        last.then_inc(s["a_th"], 1)

                    if mid and t == 20:
                        act.wait_ge(s["p_ct"], m + 1)
                        act.copy(cT2[:, :, :].rearrange("p c n -> p (c n)"), la[:, :]).then_inc(s["a_ct"], 1)
                    if mid and t == 27:
                        act.wait_ge(s["p_ht"], m + 1)
                        for ct in range(CT):
                            last = act.activation(hT[:, ct, :], la[:, ct * CH:(ct + 1) * CH], ACT.Identity,
                                                  scale=vec[:, VEC["g2"] + ct:VEC["g2"] + ct + 1],
                                                  bias=vec[:, VEC["beta2"] + ct:VEC["beta2"] + ct + 1])
                        last.then_inc(s["a_hT"], 1)

            each_iteration(act, body)

        @block.vector
        def _(dve):
            def link(chain, base, state, ins):
                state[0] += 1
                ins.then_inc(s[chain], 1)
                dve.wait_ge(s[chain], base + state[0])

            dve.memset(up_w[A:P, :], 0.0).then_inc(s["up_zero"], 1)
            for tile in (g_s, h2, ewx):
                dve.memset(tile[A:P, :], 0.0).then_inc(s["u_zero"], 1)
            dve.wait_ge(s["u_zero"], 5)
            dve.wait_ge(s["setup_in"], 16 * SETUP_LOADS)
            n = [0]
            su = lambda ins: link("setup_chain", 0, n, ins)
            su(dve.memset(h2[A:A + 1, :], 1.0))
            ef, ec, ok, bad = (sm[:, k, 0:B] for k in range(4))
            su(dve.tensor_copy(ef, e_i[:, :]))
            su(dve.tensor_scalar(ec, ef, 0.0, float(E - 1), ALU.max, ALU.min))
            su(dve.tensor_copy(idx_i[:, :], ec))
            dve.tensor_tensor(ok, ef, ec, ALU.is_equal).then_inc(s["idx_ready"], 1)
            dve.wait_ge(s["idx_ready"], 1)
            su(dve.tensor_scalar(bad, ok, -1.0, 1.0, ALU.mult, ALU.add))
            tf, q0, hi, lo, r, q1 = (sm[:, k, 0:B] for k in range(4, 10))
            inv100 = float(np.float32(1.0) / np.float32(100.0))
            su(dve.tensor_copy(tf, t_i[:, :]))
            su(dve.tensor_scalar(q0, tf, inv100, None, ALU.mult))
            su(dve.tensor_copy(tb[:, :], q0))
            su(dve.tensor_copy(hi, tb[:, :]))
            su(dve.tensor_tensor(lo, q0, hi, ALU.subtract))
            su(dve.scalar_tensor_tensor(out=r, in0=hi, scalar=-100.0, in1=tf, op0=ALU.mult, op1=ALU.add))
            su(dve.scalar_tensor_tensor(out=r, in0=lo, scalar=-100.0, in1=r, op0=ALU.mult, op1=ALU.add))
            su(dve.scalar_tensor_tensor(out=q1, in0=r, scalar=inv100, in1=q0, op0=ALU.mult, op1=ALU.add))
            su(dve.tensor_scalar(q1, q1, 4000.0, None, ALU.mult))
            arg, turn = sm[:, 10, :], sm[:, 14, :]
            freq = vec[:, VEC["freq"]:VEC["freq"] + 1]
            for j in range(2):
                su(dve.tensor_scalar(arg[:, j * B:(j + 1) * B], q1, freq, None, ALU.mult))
                su(dve.tensor_scalar(turn[:, j * B:(j + 1) * B], arg[:, j * B:(j + 1) * B],
                                     float(1 / TWO_PI), 0.25 * j, ALU.mult, ALU.add))
            su(dve.tensor_scalar(turn, turn, MAGIC, None, ALU.add))
            su(dve.tensor_scalar(turn, turn, MAGIC, None, ALU.subtract))
            for part in (C1, C2, C3):
                su(dve.scalar_tensor_tensor(out=arg, in0=turn, scalar=-part, in1=arg, op0=ALU.mult, op1=ALU.add))
            su(dve.tensor_scalar(arg[:, B:2 * B], arg[:, B:2 * B], float(np.pi / 2), None, ALU.add))
            dve.tensor_scalar(sm[:, 11, :], arg, -PI_IN, PI_IN, ALU.max, ALU.min).then_inc(s["idx_ready"], 1)
            dve.wait_ge(s["setup_act"], 2)
            su(dve.tensor_scalar(sm[:, 14, :], sm[:, 13, :], 1.0, None, ALU.add))
            su(dve.reciprocal(sm[:, 14, :], sm[:, 14, :]))
            su(dve.tensor_tensor(sm[:, 15, :], sm[:, 12, :], sm[:, 14, :], ALU.mult))
            dve.tensor_scalar(nbq[:, :], vec[:, 0:2], -0.25, None, ALU.mult)
            dve.tensor_scalar(b1g[:, :], vec[:, VEC["b1"]:VEC["b1"] + FT], GATE, None, ALU.mult)
            w2f = w2_s[:, :, :].rearrange("p c n -> p (c n)")
            su(dve.tensor_scalar(w2f, w2f, 0.5, None, ALU.mult))
            dve.wait_ge(s["expert_in"], 16 * 2 * B)
            okb = ok[0:A, :].unsqueeze(2).to_broadcast([A, B, A])
            badb = bad[0:A, :].unsqueeze(2).to_broadcast([A, B, A])
            su(dve.tensor_tensor(ew_all, ew_all, okb, ALU.mult))
            su(dve.tensor_tensor(ew_fin[:, :, 0:A], ident[0:A, 0:A].unsqueeze(1).to_broadcast([A, B, A]),
                                 badb, ALU.mult))
            su(dve.tensor_tensor(ew_fin[:, :, 0:A], ew_fin[:, :, 0:A], ew_all, ALU.add))
            su(dve.tensor_tensor(ebe[:, :, 0], ebe[:, :, 0], ok[0:A, :], ALU.mult))
            dve.tensor_tensor(ew_fin[:, :, A], ebe[:, :, 0], ebe[:, :, 1], ALU.add).then_inc(s["setup_dve"], 1)
            dve.wait_ge(s["setup_pe"], 1)
            su(dve.tensor_tensor(emb_s, lc[0:B, :], ada_r, ALU.add))
            dve.tensor_scalar(emb_s[:, 0:D], emb_s[:, 0:D], 1.0, None, ALU.add).then_inc(s["setup_dve"], 1)
            dve.wait_ge(s["setup_store"], 32)

            def row_stats(link_step, rows_in, stats, mv, done):
                for j in range(2):
                    ins = dve.bn_stats(stats[:, j, :], rows_in[:, j, :])
                link_step(ins)
                apart(dve)
                for j in range(2):
                    last = dve.bn_aggr(mv[:, j, :], stats[:, j, :])
                last.then_inc(s[done], 1)

            def body(i, attn, prev, pre, mid, ffn):
                c, m, f = i + 2, i - 2, i - 3
                n_pre, n_mid, n_ffn = [0], [0], [0]
                pre_link = lambda ins: link("pre_chain", PRE_CHAIN * c, n_pre, ins)
                mid_link = lambda ins: link("mid_chain", MID_CHAIN * m, n_mid, ins)
                ffn_link = lambda ins: link("ffn_chain", FFN_CHAIN * f, n_ffn, ins)
                for t in range(TI):
                    if attn:
                        hh, qt = t // 4, t % 4
                        dve.wait_ge(s["sc_ready"], TI * i + t + 1)
                        dve.wait_ge(s["masked"], 16 * i + 2 * hh + qt // 2 + 1)
                        apart(dve)
                        tile = bias_s[:, hh % GH, qt, :]
                        dve.tensor_tensor_reduce(out=tile, in0=sc[t % 2][:, :], in1=tile, scale=1.0, scalar=BIG,
                                                 op0=ALU.add, op1=ALU.min, accum_out=mx[:, t:t + 1]
                                                 ).then_inc(s["smax"], 1)

                    u = t - LAG_C
                    if (attn if u >= 0 else prev) and u % 2 == 0:
                        uu = u % TI
                        g = uu // 16
                        dve.wait_ge(s["pt_ready"], TI * i + u + 1)
                        if uu % 16 == 0:
                            wait(dve, s["pv_done"], 2 * i + g - 1)
                        dve.tensor_copy(pT[g][:, (uu // 4) % GH, :, (u % 4) * P:(u % 4 + 1) * P],
                                        tp[0][:, :].rearrange("p (k q) -> p k q", k=KT)).then_inc(s["copied_v"], 1)

                    if (attn if t >= 16 else prev) and t % 16 == 10:
                        g = 0 if t >= 16 else 1
                        gi = 2 * i if t >= 16 else 2 * i - 1
                        dve.wait_ge(s["probs"], 16 * (gi + 1))
                        dve.reciprocal(rinv[:, :], sums[:, 16 * g:16 * g + 16]).then_inc(s["dve_rinv"], 1)
                        dve.wait_ge(s["dve_rinv"], gi + 1)
                        dve.wait_ge(s["ctxn_tr"], gi + 1)
                        wait(dve, ctx_out[g], 16 * (i - g))
                        dve.tensor_tensor(
                            cn[g][:, :, :].rearrange("p q (h d) -> p q h d", h=GH),
                            pv[:, :].rearrange("p (q h d) -> p q h d", q=KT, h=GH)[:, :, :, 0:HD],
                            rinv[:, :].rearrange("p (h q) -> p q h", q=KT).unsqueeze(3).to_broadcast(
                                [P, KT, GH, HD]), ALU.mult).then_inc(s["ctx_norm"], 1)

                    if pre and t == 7:
                        dve.wait_ge(s["p_up"], c + 1)
                        dve.tensor_tensor(xin[:, :, :].rearrange("p j n -> p (j n)"), lb[:, :],
                                          xin[:, :, :].rearrange("p j n -> p (j n)"), ALU.add
                                          ).then_inc(s["d_x1"], 1)
                        dve.wait_ge(s["d_x1"], c + 1)
                        row_stats(pre_link, xin, st, mv0, "d_mv0")
                    if pre and t == 9:
                        dve.wait_ge(s["g_rs0"], c + 1)
                        for j in range(2):
                            ins = dve.scalar_tensor_tensor(out=xin[:, j, :], in0=xin[:, j, :], scalar=mv0[:, j, 0:1],
                                                           in1=gamma_r[:, :], op0=ALU.subtract, op1=ALU.mult)
                        pre_link(ins)
                        for j in range(2):
                            ins = dve.scalar_tensor_tensor(out=xin[:, j, :], in0=xin[:, j, :], scalar=rs0[:, j:j + 1],
                                                           in1=beta_r[:, :], op0=ALU.mult, op1=ALU.add)
                        pre_link(ins)
                        row_stats(pre_link, xin, st, mv1, "d_mv1")
                    if pre and t == 11:
                        dve.wait_ge(s["g_rs1"], c + 1)
                        wait(dve, s["p_xt1"], c)
                        wait(dve, s["g_xs"], c)
                        for j in range(2):
                            ins = dve.scalar_tensor_tensor(out=xin[:, j, :], in0=xin[:, j, :], scalar=mv1[:, j, 0:1],
                                                           in1=mod[:, 0:D], op0=ALU.subtract, op1=ALU.mult)
                        pre_link(ins)
                        for j in range(2):
                            last = dve.scalar_tensor_tensor(out=xm[:, j, :], in0=xin[:, j, :], scalar=rs1[:, j:j + 1],
                                                            in1=mod[:, D:2 * D], op0=ALU.mult, op1=ALU.add)
                        last.then_inc(s["d_xm"], 1)
                    if pre and t == 18:
                        dve.wait_ge(s["p_v"], c + 1)
                        wait(dve, s["qkv_out"], 16 * QKV_STORES * c)
                        dve.tensor_tensor(vs[:, :, :], lb[:, :].rearrange("p (j n) -> p j n", j=2),
                                          bv_r[:, :].unsqueeze(1).to_broadcast([P, 2, D]), ALU.add
                                          ).then_inc(s["d_v"], 1)
                        dve.wait_ge(s["a_k"], c + 1)
                        pre_link(dve.tensor_copy(qkb[:, 0, :], qk[:, :]))
                        pre_link(dve.tensor_tensor(qk[:, :], qk[:, :], qkb[:, 0, :], ALU.subtract))
                    if pre and t == 19:
                        pre_link(dve.tensor_copy(qkb[:, 1, :], qk[:, :]))
                        dve.tensor_tensor(qkb[:, 2, :], qk[:, :], qkb[:, 1, :], ALU.subtract
                                          ).then_inc(s["d_split"], 1)

                    if ffn and t in (3, 6, 9, 12):
                        p = t // 3 - 1
                        dve.wait_ge(s["a_th"], 4 * f + p + 1)
                        if p == 0:
                            wait(dve, s["p_w2"], 4 * f)
                        ffn_link(dve.tensor_scalar(th[:, :], th[:, :], 1.0, None, ALU.add))
                        for n in range(2):
                            ft = 2 * p + n
                            last = dve.scalar_tensor_tensor(
                                out=act_s[:, ft, :], in0=lc[:, n * CH:(n + 1) * CH],
                                scalar=vec[:, VEC["b1"] + ft:VEC["b1"] + ft + 1],
                                in1=th[:, n * CH:(n + 1) * CH], op0=ALU.add, op1=ALU.mult)
                        last.then_inc(s["d_act"], 1)
                    if ffn and t == 20:
                        dve.wait_ge(s["p_w2"], 4 * f + 4)
                        dve.wait_ge(s["g_x2b"], f + 1)
                        dve.tensor_tensor(x2b[:, :, :].rearrange("p j n -> p (j n)"), lc[:, :],
                                          x2b[:, :, :].rearrange("p j n -> p (j n)"), ALU.add
                                          ).then_inc(s["d_out"], 1)

                    if mid and t == 22:
                        dve.wait_ge(s["p_wo"], m + 1)
                        wait(dve, s["g_x2b"], m)
                        dve.tensor_tensor(x2[:, :, :].rearrange("p j n -> p (j n)"), lb[:, :],
                                          xsin[:, :, :].rearrange("p j n -> p (j n)"), ALU.add
                                          ).then_inc(s["d_x2"], 1)
                        dve.wait_ge(s["d_x2"], m + 1)
                        row_stats(mid_link, x2, st2, mv2, "d_mv2")
                    if mid and t == 25:
                        dve.wait_ge(s["g_rs2"], m + 1)
                        for j in range(2):
                            last = dve.tensor_scalar(xsin[:, j, :], x2[:, j, :], mv2[:, j, 0:1], rs2[:, j:j + 1],
                                                     ALU.subtract, ALU.mult)
                        last.then_inc(s["d_hn"], 1)
                assert not pre or n_pre[0] == PRE_CHAIN, n_pre
                assert not mid or n_mid[0] == MID_CHAIN, n_mid
                assert not ffn or n_ffn[0] == FFN_CHAIN, n_ffn

            each_iteration(dve, body)


def kernel(**inputs):
    import concourse.bacc as bacc
    from concourse.bass_utils import run_bass_kernel_spmd

    def get(name):
        return np.asarray(inputs[name])

    def tiles(v, n):
        return v.reshape(n, P).T

    def by_head(w):
        return w.reshape(-1, 8, 2, HD).transpose(0, 2, 3, 1).reshape(-1, D)

    freqs = np.exp(np.arange(P, dtype=np.float32) * np.float32(-np.log(10000.0) / (P - 1))).astype(np.float32)
    down_b = np.concatenate([get("L0_cond_down_b"), np.zeros(P - A, np.float32)])
    vecs = np.concatenate([
        tiles(by_head(get("L1_cond_bq")[None])[0], 2), tiles(by_head(get("L1_cond_bk")[None])[0], 2),
        tiles(get("L1_cond_g2"), 2), tiles(get("L1_cond_beta2"), 2), tiles(get("L1_cond_b1"), FT),
        down_b[:, None], freqs[:, None]], axis=1)
    arrays = {
        "x": get("x").reshape(B * S, D),
        "t_tok": get("itok_B_34_63").reshape(1, B),
        "e_tok": get("itok_B_0_15").reshape(1, B),
        "bias": get("fside_Bx16xSxS_0").reshape(B * H, S, S),
        "mask": get("mask_Bx1xSxS_bk0").reshape(B, S, S),
        "downT": get("L0_cond_down_W").T,
        "upT": get("L0_cond_up_W").T,
        "up_b": get("L0_cond_up_b")[None],
        "expertT": get("L0_cond_expert_W").transpose(0, 2, 1),
        "expert_be": np.stack([get("L0_cond_expert_b"), get("L0_cond_domain_emb")], axis=2),
        "gamma": get("L0_cond_ln_gamma")[None],
        "beta": get("L0_cond_ln_beta")[None],
        "w_ada": get("L1_cond_W_ada"),
        "b_ada": get("L1_cond_b_ada")[None],
        "wq": by_head(get("L1_cond_Wq")),
        "wk": by_head(get("L1_cond_Wk")),
        "wv": get("L1_cond_Wv"),
        "bv": get("L1_cond_bv")[None],
        "wo": get("L1_cond_Wo"),
        "bo": get("L1_cond_bo")[None],
        "w1": get("L1_cond_W1"),
        "w2": get("L1_cond_W2"),
        "b2": get("L1_cond_b2")[None],
        "vecs": vecs,
        "ident_in": np.eye(P, dtype=np.float32),
    }
    nc = bacc.Bacc("TRN2", target_bir_lowering=False, num_devices=1)
    feed, aps = {}, {}
    for name, a in arrays.items():
        a = np.ascontiguousarray(a)
        feed[f"in_{name}"] = a
        aps[name] = nc.dram_tensor(f"in_{name}", a.shape, mybir.dt.from_np(a.dtype), kind="ExternalInput").ap()
    out = nc.dram_tensor("out_rows", (B * S, D), F32, kind="ExternalOutput").ap()
    build(nc, *aps.values(), out)
    got = run_bass_kernel_spmd(nc, [feed], core_ids=[0])
    return got.results[0]["out_rows"].reshape(B, S, D)
```

```python
from contextlib import ExitStack

import numpy as np

import concourse.bass as bass
from concourse import mybir

F32 = mybir.dt.float32
BF16 = mybir.dt.bfloat16
I32 = mybir.dt.int32
U8 = mybir.dt.uint8
ALU = mybir.AluOpType
ACT = mybir.ActivationFunctionType

P = 128
B, S, D = 8, 512, 256
H, HD = 16, 16
A, E = 64, 16
F = 1024
EPS = 1e-5
CH = 256
NCH = B * S // CH
CT = D // P
FT = F // P
GH = 4
TI = 32
KT = S // P
LAG = 4
PV_AT, CTXT_AT, CTXN_AT, NORM_AT = 6, 10, 13, 14
MASKED = 1e30
BIG = 3.0e38
K_SLOTS = 5
RUNS = [(0, 3, 1), (48, 3, 2), (96, 2, 0)]
W1_AT = (3, 4, 8, 9, 13, 14, 16, 17)
TANH_AT, GATE_AT = (5, 10, 15, 18), (6, 11, 16, 19)
W2_AT = (19, 20, 21, 26, 27, 28, 29, 30)
SPLIT_Q, SPLIT_K = (3, 4, 8, 10), (14, 15, 17, 18)
GATE = 1.702 / 2
FIRST, LAST = -3, NCH + 2
PRE_CHAIN, QKV_CHAIN, MID_CHAIN, FFN_CHAIN = 5, 6, 1, 4
VEC = {"bq": 0, "bk": 2, "g2": 4, "beta2": 6, "b1": 8, "down_b": 16, "freq": 17}
TWO_PI = 2 * np.pi
C1 = 6.28125
C2 = float(np.round((TWO_PI - C1) * 2**21) / 2**21)
C3 = float(TWO_PI - C1 - C2)
MAGIC = 1.5 * 2.0**23
PI_IN = 3.1415925


def stages(i):
    return dict(attn=0 <= i < NCH, prev=1 <= i <= NCH, nxt=0 <= i + 1 < NCH, pre=0 <= i + 3 < NCH,
                qkv=0 <= i + 2 < NCH, mid=0 <= i - 2 < NCH, ffn=0 <= i - 3 < NCH)


def wait(eng, sem, value):
    if isinstance(value, int) and value <= 0:
        return
    eng.wait_ge(sem, value)


def apart(eng):
    eng.nop(nofuse=True)


def each_iteration(eng, body):
    for i in range(FIRST, 3):
        body(i, **stages(i))
    with eng.Fori(3, NCH - 3) as i:
        body(i, **stages(3))
    for i in range(NCH - 3, LAST + 1):
        body(i, **stages(i))


def build(nc, x, t_tok, e_tok, bias, mask, downT, upT, up_b, expertT, expert_be, gamma, beta,
          w_ada, b_ada, wq, wk, wv, bv, wo, bo, w1, w2, b2, vecs, ident_in, out):
    x_v = x.rearrange("(c j p) d -> c p j d", j=2, p=P)
    out_v = out.rearrange("(c j p) d -> c p j d", j=2, p=P)
    bias_v = bias.rearrange("h (q p) k -> h p q k", p=P)
    mask_v = mask.rearrange("b (q p) k -> b p q k", p=P)

    def dram(name, shape, dt):
        return nc.dram_tensor(name, shape, dt, kind="Internal").ap()

    q_d = dram("q_parts", (B, H, 3 * HD, S), BF16)
    k_d = dram("k_parts", (B, H, K_SLOTS * HD, S), BF16)
    v_d = dram("v_rows", (B * S, D), F32)
    xs_d = dram("x_rows", (B * S, D), F32)
    ctx_d = dram("ctx_rows", (B * S, D), F32)
    emb_d = dram("emb_rows", (B, 2 * D), F32)
    ew_d = dram("expert_rows", (B, A, A + 1), F32)
    xs_v = xs_d.rearrange("(c j p) d -> c p j d", j=2, p=P)
    ctx_v = ctx_d.rearrange("(c j p) d -> c p j d", j=2, p=P)
    v_v = v_d.rearrange("(c j p) d -> c p j d", j=2, p=P)
    v_b = v_d.rearrange("(b k p) d -> b p k d", k=KT, p=P)
    ctx_b = ctx_d.rearrange("(b k p) d -> b p k d", k=KT, p=P)

    with ExitStack() as ctx:
        def sb(name, shape, dt=F32):
            return ctx.enter_context(nc.sbuf_tensor(name, shape, dt))

        def ps(name):
            return ctx.enter_context(nc.psum_tensor(name, [P, 512], F32))

        def sem(name):
            return ctx.enter_context(nc.semaphore(name))

        ident = sb("ident", [P, P])
        down_w = sb("down_w", [P, CT, A])
        up_w = sb("up_w", [P, D])
        wq_s = sb("wq_s", [P, CT, D])
        wk_s = sb("wk_s", [P, CT, D])
        wv_s = sb("wv_s", [P, CT, D])
        wo_s = sb("wo_s", [P, CT, D])
        w1_s = sb("w1_s", [P, CT, F])
        w2_s = sb("w2_s", [P, FT, D])
        gamma_r = sb("gamma_r", [P, D])
        beta_r = sb("beta_r", [P, D])
        bo_r = sb("bo_r", [P, D])
        bv_r = sb("bv_r", [P, D])
        b2_r = sb("b2_r", [P, D])
        vec = sb("vec", [P, 18])
        nbq = sb("nbq", [P, 2])
        b1g = sb("b1g", [P, FT])
        powc = sb("powc", [P, 2])

        bias_s = sb("bias_s", [P, GH, KT, S])
        mask_raw = sb("mask_raw", [P, KT, S], U8)
        mask_f = sb("mask_f", [P, KT, S])
        stq = [sb(f"stq{g}", [P, GH, S], BF16) for g in range(2)]
        stk = [sb(f"stk{g}", [P, GH, S], BF16) for g in range(2)]
        v_s = [sb(f"v_s{g}", [P, KT, GH * HD + HD]) for g in range(2)]
        pT = [sb(f"pT{g}", [P, GH, KT, S]) for g in range(2)]
        mx = sb("mx", [P, TI])
        sums = sb("sums", [P, TI])
        rinv = sb("rinv", [P, 16])
        cT = sb("cT", [P, S])
        cn = [sb(f"cn{g}", [P, KT, GH * HD]) for g in range(2)]

        xin = sb("xin", [P, 2, D])
        xT = sb("xT", [P, CT, CH])
        xT1 = sb("xT1", [P, CT, CH])
        g_s = sb("g_s", [P, CH])
        h2 = sb("h2", [P, CH])
        ewx = sb("ewx", [P, A + 1])
        mod = sb("mod", [P, 2 * D])
        xm = sb("xm", [P, 2, D])
        xs = sb("xs", [P, 2, D])
        qk = sb("qk", [P, 2 * CH])
        qkb = sb("qkb", [P, 3, 4 * CH], BF16)
        vs = sb("vs", [P, 2, D])
        st = sb("st", [P, 2, 6])
        mv0 = sb("mv0", [P, 2, 2])
        mv1 = sb("mv1", [P, 2, 2])
        rs0 = sb("rs0", [P, 2])
        rs1 = sb("rs1", [P, 2])

        cin = sb("cin", [P, 2, D])
        xsin = sb("xsin", [P, 2, D])
        cT2 = sb("cT2", [P, CT, CH])
        x2 = sb("x2", [P, 2, D])
        x2b = sb("x2b", [P, 2, D])
        hT = sb("hT", [P, CT, CH])
        st2 = sb("st2", [P, 2, 6])
        mv2 = sb("mv2", [P, 2, 2])
        rs2 = sb("rs2", [P, 2])
        th = sb("th", [P, 2 * CH])
        act_s = sb("act_s", [P, FT, CH])

        t_i = sb("t_i", [P, B], I32)
        e_i = sb("e_i", [P, B], I32)
        idx_i = sb("idx_i", [P, B], I32)
        sm = sb("sm", [P, 16, 2 * B])
        tb = sb("tb", [P, B], BF16)
        w_ada_s = pT[0][:, 0, 0:2, :]
        ew_all = pT[0][0:A, 1, 0:1, :].rearrange("p a (b o) -> p (a b) o", b=B)
        ew_fin = pT[0][0:A, 2, 0:2, :].rearrange("p a n -> p (a n)")[:, 0:B * (A + 1)].rearrange(
            "p (b o) -> p b o", b=B)
        ebe = pT[0][0:A, 3, 0, 0:2 * B].rearrange("p (b o) -> p b o", b=B)
        ada_r = pT[0][0:B, 1, 1, :]
        emb_s = pT[0][0:B, 1, 2, :]

        sc = [ps("sc0"), ps("sc1")]
        tp = [ps("tp0"), ps("tp1")]
        pv = ps("pv")
        la, lb, lc = ps("la"), ps("lb"), ps("lc")

        def w1_bank(p):
            return pv if p == 3 else lc

        names = """setup_in up_zero u_zero setup_chain setup_dve setup_act setup_pe idx_ready expert_in setup_store
            mask_in mask_ready masked sc_ready smax probs pt_ready copied_v copied_a pv_done ctxT_ready
            ctxn_tr ctx_norm dve_rinv x_in p_xt a_xt p_down a_gelu p_exp a_h2 p_up d_x1 d_mv0 g_rs0
            mod_in d_mv1 g_rs1 d_xm p_xt1 a_xt1 p_q p_k a_q a_k d_qs d_ks p_v d_v g_xs xs_out qkv_out pre_chain
            pool_pre cx_in p_ct a_ct p_wo d_x2 d_mv2 g_rs2 g_x2b d_hn p_ht a_hT mid_chain pool_mid
            p_w1 a_th d_act p_w2 d_out ffn_chain qkv_chain out_out""".split()
        s = {n: sem(n) for n in names}
        bias_in = [sem(f"bias_in{n}") for n in range(GH)]
        stack_in = [sem(f"stack_in{g}") for g in range(2)]
        v_in = [sem(f"v_in{g}") for g in range(2)]
        ctx_out = [sem(f"ctx_out{g}") for g in range(2)]
        SETUP_LOADS = 20
        STACK_LOADS = 6
        QKV_STORES = 3 + K_SLOTS + 1

        block = ctx.enter_context(nc.Block())

        @block.sync
        def _(sp):
            def wait(eng, sem, value):
                if isinstance(value, int) and value <= 0:
                    return
                eng.wait_ge(sem, value)
                if not isinstance(value, int):
                    apart(eng)

            def load_bias(i, hh):
                wait(sp, s["pt_ready"], TI * i + 4 * hh - 12)
                sp.dma_start(bias_s[:, hh % GH, :, :],
                             bias_v[bass.ds(8 * i + hh, 1)].rearrange("h p q k -> (h p) q k")
                             ).then_inc(bias_in[hh % GH], 16)

            def load_mask(i):
                wait(sp, s["mask_ready"], i)
                sp.dma_start(mask_raw[:, :, :],
                             mask_v[bass.ds(i // 2, 1)].rearrange("b p q k -> (b p) q k")
                             ).then_inc(s["mask_in"], 16)

            def load_stack(i, g):
                head = (i % 2) * 8 + GH * g
                wait(sp, s["sc_ready"], TI * (i - 1) + 16 * (g + 1))
                for row, parts, k0 in RUNS:
                    n = parts * HD
                    qsrc = q_d[bass.ds(i // 2, 1), bass.ds(head, GH), 0:n, :]
                    ksrc = k_d[bass.ds(i // 2, 1), bass.ds(head, GH), k0 * HD:k0 * HD + n, :]
                    sp.dma_start(stq[g][row:row + n], qsrc.rearrange("b h r t -> (b r) h t")
                                 ).then_inc(stack_in[g], 16)
                    sp.dma_start(stk[g][row:row + n], ksrc.rearrange("b h r t -> (b r) h t")
                                 ).then_inc(stack_in[g], 16)

            def load_v(i, g):
                wait(sp, s["pv_done"], 2 * (i - 1) + g + 1)
                col = ((i % 2) * 8 + GH * g) * HD
                sp.dma_start(v_s[g][:, :, 0:GH * HD],
                             v_b[bass.ds(i // 2, 1), :, :, bass.ds(col, GH * HD)].rearrange(
                                 "b p k d -> (b p) k d")).then_inc(v_in[g], 16)

            def store_ctx(i, g):
                wait(sp, s["ctx_norm"], 2 * i + g + 1)
                col = ((i % 2) * 8 + GH * g) * HD
                sp.dma_start(ctx_b[bass.ds(i // 2, 1), :, :, bass.ds(col, GH * HD)].rearrange(
                    "b p k d -> (b p) k d"), cn[g][:, :, :]).then_inc(ctx_out[g], 16)

            def rows(view, c):
                return view[bass.ds(c, 1)].rearrange("c p j d -> (c p) j d")

            loads = [(ident[:, :], ident_in), (down_w[:, :, :], downT.rearrange("(c p) a -> p c a", p=P)),
                     (up_w[0:A, :], upT), (wq_s[:, :, :], wq.rearrange("(c p) n -> p c n", p=P)),
                     (wk_s[:, :, :], wk.rearrange("(c p) n -> p c n", p=P)),
                     (wv_s[:, :, :], wv.rearrange("(c p) n -> p c n", p=P)),
                     (wo_s[:, :, :], wo.rearrange("(c p) n -> p c n", p=P)),
                     (w1_s[:, :, :], w1.rearrange("(c p) n -> p c n", p=P)),
                     (w2_s[:, :, :], w2.rearrange("(c p) n -> p c n", p=P)),
                     (w_ada_s, w_ada.rearrange("(c p) n -> p c n", p=P)),
                     (gamma_r[:, :], gamma.to_broadcast([P, D])), (beta_r[:, :], beta.to_broadcast([P, D])),
                     (bo_r[:, :], bo.to_broadcast([P, D])), (bv_r[:, :], bv.to_broadcast([P, D])),
                     (b2_r[:, :], b2.to_broadcast([P, D])), (vec[:, :], vecs),
                     (ada_r, b_ada.to_broadcast([B, 2 * D])),
                     (t_i[:, :], t_tok.to_broadcast([P, B])), (e_i[:, :], e_tok.to_broadcast([P, B]))]
            for dst, src in loads:
                sp.dma_start(dst, src).then_inc(s["setup_in"], 16)
            sp.wait_ge(s["up_zero"], 1)
            sp.dma_start(up_w[A:A + 1, :], up_b).then_inc(s["setup_in"], 16)
            sp.wait_ge(s["idx_ready"], 1)
            sp.wait_ge(s["setup_in"], 16 * SETUP_LOADS)
            for b in range(B):
                e = sp.value_load(idx_i[0:1, b:b + 1], min_val=0, max_val=E - 1)
                sp.dma_start(ew_all[:, b, :], expertT[bass.ds(e, 1)].rearrange("e a o -> (e a) o")
                             ).then_inc(s["expert_in"], 16)
                sp.dma_start(ebe[:, b, :], expert_be[bass.ds(e, 1)].rearrange("e a o -> (e a) o")
                             ).then_inc(s["expert_in"], 16)
            sp.wait_ge(s["setup_dve"], 1)
            sp.dma_start(ew_d.rearrange("b a o -> a b o"), ew_fin).then_inc(s["setup_store"], 16)
            sp.wait_ge(s["setup_dve"], 2)
            sp.dma_start(emb_d, emb_s).then_inc(s["setup_store"], 16)
            sp.wait_ge(s["setup_store"], 32)

            def store_parts(c, dst, slot, part, off):
                sp.dma_start(
                    dst[bass.ds(c // 2, 1), :, slot * HD:(slot + 1) * HD,
                        bass.ds((c % 2) * CH, CH)].rearrange("b h d t -> (b d) h t"),
                    qkb[:, part, off:off + 2 * CH].rearrange("p (m t) -> p m t", m=2)
                ).then_inc(s["qkv_out"], 16)

            def body(i, attn, prev, nxt, pre, qkv, mid, ffn):
                a, c, m, f = i + 3, i + 2, i - 2, i - 3
                if pre:
                    wait(sp, s["d_xm"], a)
                    sp.dma_start(xin[:, :, :], rows(x_v, a)).then_inc(s["x_in"], 16)
                    wait(sp, s["p_exp"], a)
                    wait(sp, s["a_h2"], a)
                    sp.dma_start(ewx[0:A, :], ew_d[bass.ds(a // 2, 1)].rearrange("b a o -> (b a) o")
                                 ).then_inc(s["x_in"], 16)
                    sp.dma_start(mod[:, :], emb_d[bass.ds(a // 2, 1)].to_broadcast([P, 2 * D])
                                 ).then_inc(s["mod_in"], 16)
                if attn:
                    load_stack(i, 1)
                    load_bias(i, 3)
                    load_bias(i, 4)
                if qkv:
                    wait(sp, s["d_v"], c + 1)
                    sp.dma_start(rows(v_v, c), vs[:, :, :]).then_inc(s["qkv_out"], 16)
                if attn:
                    load_v(i, 1)
                if qkv:
                    wait(sp, s["d_qs"], c + 1)
                    for n in range(3):
                        store_parts(c, q_d, n, n, 0)
                if attn:
                    load_bias(i, 5)
                if prev:
                    store_ctx(i - 1, 1)
                if attn:
                    load_bias(i, 6)
                if nxt:
                    load_mask(i + 1)
                if mid:
                    for g in range(2):
                        wait(sp, ctx_out[g], 16 * i if prev else 16 * NCH)
                    wait(sp, s["xs_out"], 16 * (i + 3) if qkv else 16 * NCH)
                    wait(sp, s["p_ct"], m)
                    wait(sp, s["p_ht"], m)
                    sp.dma_start(cin[:, :, :], rows(ctx_v, m)).then_inc(s["cx_in"], 16)
                    sp.dma_start(xsin[:, :, :], rows(xs_v, m)).then_inc(s["cx_in"], 16)
                if qkv:
                    wait(sp, s["d_ks"], c + 1)
                    for n in range(K_SLOTS):
                        store_parts(c, k_d, n, n % 3, 2 * CH)
                if attn:
                    load_bias(i, 7)
                if nxt:
                    wait(sp, s["qkv_out"], 16 * QKV_STORES * (c + 1 if qkv else NCH))
                    load_stack(i + 1, 0)
                    load_bias(i + 1, 0)
                    load_v(i + 1, 0)
                    load_bias(i + 1, 1)
                if pre:
                    wait(sp, s["g_xs"], a + 1)
                    sp.dma_start(rows(xs_v, a), xs[:, :, :]).then_inc(s["xs_out"], 16)
                if attn:
                    store_ctx(i, 0)
                if nxt:
                    load_bias(i + 1, 2)
                if ffn:
                    wait(sp, s["d_out"], f + 1)
                    sp.dma_start(rows(out_v, f), x2b[:, :, :]).then_inc(s["out_out"], 16)

            each_iteration(sp, body)
            sp.wait_ge(s["out_out"], 16 * NCH)
            sp.wait_ge(s["xs_out"], 16 * NCH)
            sp.wait_ge(s["qkv_out"], 16 * QKV_STORES * NCH)
            for g in range(2):
                sp.wait_ge(ctx_out[g], 16 * NCH)

        @block.gpsimd
        def _(pool):
            pool.memset(powc[:, :], -0.5).then_inc(s["pool_pre"], 1)
            pool.memset(v_s[0][:, :, :], 0.0).then_inc(s["u_zero"], 1)
            pool.memset(v_s[1][:, :, :], 0.0).then_inc(s["u_zero"], 1)
            pool.wait_ge(s["pool_pre"], 1)
            pool.wait_ge(s["setup_in"], 16 * SETUP_LOADS)

            def mask_head(i, hh, halves=(0, 1)):
                if 0 in halves:
                    pool.wait_ge(bias_in[hh % GH], 16 * (2 * i + hh // GH + 1))
                for half in halves:
                    b = bias_s[:, hh % GH, 2 * half:2 * half + 2, :]
                    pool.tensor_tensor(b, mask_f[:, 2 * half:2 * half + 2, :], b, ALU.subtract
                                       ).then_inc(s["masked"], 1)

            def rsqrt(chain, base, var, dst):
                apart(pool)
                pool.tensor_scalar(dst, var, EPS, 1.0, ALU.add, ALU.mult).then_inc(s[chain], 1)
                pool.wait_ge(s[chain], base)
                return pool.tensor_tensor(dst, dst, powc[:, :], ALU.pow)

            def body(i, attn, prev, nxt, pre, qkv, mid, ffn):
                a, m, f = i + 3, i - 2, i - 3
                if attn:
                    mask_head(i, 1)
                    mask_head(i, 2)
                if ffn:
                    pool.wait_ge(s["d_x2"], f + 1)
                    wait(pool, s["out_out"], 16 * f)
                    pool.tensor_tensor(x2b[:, :, :], x2[:, :, :],
                                       b2_r[:, :].unsqueeze(1).to_broadcast([P, 2, D]), ALU.add
                                       ).then_inc(s["g_x2b"], 1)
                if attn:
                    for hh in range(3, 7):
                        mask_head(i, hh)
                if pre:
                    pool.wait_ge(s["d_mv0"], a + 1)
                    wait(pool, s["d_mv1"], a)
                    rsqrt("pool_pre", 2 * a + 2, mv0[:, :, 1], rs0[:, :]).then_inc(s["g_rs0"], 1)
                if attn:
                    mask_head(i, 7)
                if pre:
                    pool.wait_ge(s["d_mv1"], a + 1)
                    wait(pool, s["d_xm"], a)
                    rsqrt("pool_pre", 2 * a + 3, mv1[:, :, 1], rs1[:, :]).then_inc(s["g_rs1"], 1)
                if nxt:
                    pool.wait_ge(s["mask_in"], 16 * (i + 2))
                    wait(pool, s["masked"], 16 * (i + 1))
                    apart(pool)
                    pool.tensor_scalar(mask_f[:, :, :], mask_raw[:, :, :], MASKED, 0.0, ALU.mult, ALU.add
                                       ).then_inc(s["mask_ready"], 1)
                    pool.wait_ge(s["mask_ready"], i + 2)
                    mask_head(i + 1, 0, (0,))
                if mid:
                    pool.wait_ge(s["d_mv2"], m + 1)
                    wait(pool, s["d_hn"], m)
                    rsqrt("pool_mid", m + 1, mv2[:, :, 1], rs2[:, :]).then_inc(s["g_rs2"], 1)
                if nxt:
                    mask_head(i + 1, 0, (1,))
                if pre:
                    pool.wait_ge(s["d_xm"], a + 1)
                    wait(pool, s["xs_out"], 16 * a)
                    pool.tensor_tensor(xs[:, :, :], xm[:, :, :],
                                       bo_r[:, :].unsqueeze(1).to_broadcast([P, 2, D]), ALU.add
                                       ).then_inc(s["g_xs"], 1)

            each_iteration(pool, body)

        @block.tensor
        def _(pe):
            def transposes(dst, src, done):
                for ct in range(CT):
                    for j in range(2):
                        last = pe.transpose(dst[:, ct * CH + j * P:ct * CH + (j + 1) * P],
                                            src[:, j, ct * P:(ct + 1) * P], ident[:, :])
                last.then_inc(s[done], 1)

            pe.wait_ge(s["setup_in"], 16 * SETUP_LOADS)
            pe.wait_ge(s["setup_dve"], 1)
            for j in range(2):
                last = pe.matmul(lc[0:B, :], sm[:, 15, j * B:(j + 1) * B], w_ada_s[:, j, :],
                                 start=(j == 0), stop=(j == 1))
            last.then_inc(s["setup_pe"], 1)
            pe.wait_ge(s["setup_dve"], 2)
            pe.wait_ge(s["u_zero"], 5)

            def body(i, attn, prev, nxt, pre, qkv, mid, ffn):
                a, c, m, f = i + 3, i + 2, i - 2, i - 3
                for t in range(TI):
                    if attn:
                        hh, qt = t // 4, t % 4
                        g = hh // GH
                        if t % 16 == 0:
                            pe.wait_ge(stack_in[g], 16 * STACK_LOADS * (i + 1))
                        wait(pe, s["smax"], TI * i + t - 1)
                        pe.matmul(sc[t % 2][:, :], stq[g][:, hh % GH, qt * P:(qt + 1) * P],
                                  stk[g][:, hh % GH, :], start=True, stop=True).then_inc(s["sc_ready"], 1)

                    if qkv and t in (0, 1, 11, 12):
                        w, dst, done = (wq_s, lb, "p_q") if t < 2 else (wk_s, la, "p_k")
                        mt = t if t < 2 else t - 11
                        if t == 0:
                            pe.wait_ge(s["a_xt1"], c + 1)
                            wait(pe, s["d_x2"], m)
                        if t == 11 and not pre and ffn:
                            pe.wait_ge(s["a_hT"], f + 1)
                        for ct in range(CT):
                            last = pe.matmul(dst[:, mt * CH:(mt + 1) * CH], w[:, ct, mt * P:(mt + 1) * P],
                                             xT1[:, ct, :], start=(ct == 0), stop=(ct == CT - 1))
                        if mt == 1:
                            last.then_inc(s[done], 1)
                    if qkv and t in (4, 5):
                        j = t - 4
                        if j == 0:
                            pe.wait_ge(s["a_q"], c + 1)
                        for ct in range(CT):
                            last = pe.matmul(lb[:, j * D:(j + 1) * D], xT1[:, ct, j * P:(j + 1) * P],
                                             wv_s[:, ct, :], start=(ct == 0), stop=(ct == CT - 1))
                        if j == 1:
                            last.then_inc(s["p_v"], 1)

                    if pre and t == 3:
                        pe.wait_ge(s["x_in"], 32 * (a + 1))
                        wait(pe, s["a_hT"], f + 1)
                        transposes(la, xin, "p_xt")
                    if pre and t == 10:
                        pe.wait_ge(s["a_xt"], a + 1)
                        wait(pe, s["d_v"], c + 1)
                        for ct in range(CT):
                            last = pe.matmul(lb[0:A, 0:CH], down_w[:, ct, :], xT[:, ct, :],
                                             start=(ct == 0), stop=(ct == CT - 1))
                        last.then_inc(s["p_down"], 1)
                    if pre and t == 15:
                        pe.wait_ge(s["a_gelu"], a + 1)
                        wait(pe, s["a_k"], c + 1)
                        pe.matmul(la[0:A, 0:CH], ewx[:, 0:A], g_s[:, :], start=True, stop=True
                                  ).then_inc(s["p_exp"], 1)
                    if pre and t == 18:
                        pe.wait_ge(s["a_h2"], a + 1)
                        for j in range(2):
                            last = pe.matmul(lb[:, j * D:(j + 1) * D], h2[:, j * P:(j + 1) * P], up_w[:, :],
                                             start=True, stop=True)
                        last.then_inc(s["p_up"], 1)
                    if pre and t == 28:
                        pe.wait_ge(s["d_xm"], a + 1)
                        transposes(la, xm, "p_xt1")

                    if ffn and t in W1_AT:
                        ft = W1_AT.index(t)
                        bank = w1_bank(ft // 2)
                        if ft == 0:
                            pe.wait_ge(s["a_hT"], f + 1)
                            wait(pe, s["d_out"], f)
                        if ft in (2, 4):
                            pe.wait_ge(s["d_act"], 4 * f + ft // 2)
                        if ft == 6:
                            wait(pe, s["ctx_norm"], 2 * i if prev else 2 * NCH)
                        for ct in range(CT):
                            last = pe.matmul(bank[:, (ft % 2) * CH:(ft % 2 + 1) * CH],
                                             w1_s[:, ct, ft * P:(ft + 1) * P],
                                             hT[:, ct, :], start=(ct == 0), stop=(ct == CT - 1))
                        if ft % 2 == 1:
                            last.then_inc(s["p_w1"], 1)
                    for r in range(8):
                        if ffn and t == W2_AT[r]:
                            j = r // 4
                            if j == 0:
                                pe.wait_ge(s["d_act"], 4 * f + max(3, r + 1))
                            for ft in range(2 * (r % 4), 2 * (r % 4) + 2):
                                last = pe.matmul(lc[:, j * D:(j + 1) * D], act_s[:, ft, j * P:(j + 1) * P],
                                                 w2_s[:, ft, :], start=(ft == 0), stop=(ft == FT - 1))
                            if r == 7:
                                last.then_inc(s["p_w2"], 1)

                    if mid and t == 20:
                        pe.wait_ge(s["cx_in"], 32 * (m + 1))
                        if qkv and not pre:
                            pe.wait_ge(s["a_k"], c + 1)
                        transposes(la, cin, "p_ct")
                    if mid and t in (23, 24):
                        j = t - 23
                        if j == 0:
                            pe.wait_ge(s["a_ct"], m + 1)
                            if pre:
                                pe.wait_ge(s["d_x1"], a + 1)
                            elif qkv:
                                pe.wait_ge(s["d_v"], c + 1)
                            else:
                                wait(pe, s["d_x2"], m)
                        for ct in range(CT):
                            last = pe.matmul(lb[:, j * D:(j + 1) * D], cT2[:, ct, j * P:(j + 1) * P],
                                             wo_s[:, ct, :], start=(ct == 0), stop=(ct == CT - 1))
                        if j == 1:
                            last.then_inc(s["p_wo"], 1)
                    if mid and t == 31:
                        pe.wait_ge(s["d_hn"], m + 1)
                        if pre:
                            pe.wait_ge(s["a_xt1"], a + 1)
                        transposes(la, xsin, "p_ht")

                    u = t - LAG
                    if attn if u >= 0 else prev:
                        pe.wait_ge(s["probs"], TI * i + u + 1)
                        wait(pe, s["copied_a" if u % 2 else "copied_v"], 16 * i + u // 2)
                        src = bias_s[:, (u // 4) % GH, u % 4, :]
                        for kt in range(KT):
                            last = pe.transpose(tp[u % 2][:, kt * P:(kt + 1) * P],
                                                src[:, kt * P:(kt + 1) * P], ident[:, :])
                        last.then_inc(s["pt_ready"], 1)

                    g = 0 if t >= 16 else 1
                    gi = 2 * i + g if g == 0 else 2 * i - 1
                    kt = t % 16 - PV_AT
                    if (attn if g == 0 else prev) and kt in range(KT):
                        if kt == 0:
                            pe.wait_ge(s["copied_v"], 8 * (gi + 1))
                            pe.wait_ge(s["copied_a"], 8 * (gi + 1))
                            pe.wait_ge(v_in[g], 16 * (i + 1 - g))
                            wait(pe, s["ctx_norm"], gi)
                            if ffn and g == 0:
                                pe.wait_ge(s["d_act"], 4 * f + 4)
                        for h in range(GH):
                            last = pe.matmul(pv[32 * h:32 * h + 32, :], v_s[g][:, kt, HD * h:HD * h + 32],
                                             pT[g][:, h, kt, :], start=(kt == 0), stop=(kt == KT - 1),
                                             tile_position=(0, 32 * h))
                        if kt == KT - 1:
                            last.then_inc(s["pv_done"], 1)
                    if (attn if g == 0 else prev) and t % 16 == CTXN_AT:
                        pe.wait_ge(s["ctxT_ready"], gi + 1)
                        for qt in range(KT):
                            last = pe.transpose(pv[:, qt * P:(qt + 1) * P], cT[:, qt * P:(qt + 1) * P],
                                                ident[:, :])
                        last.then_inc(s["ctxn_tr"], 1)

            each_iteration(pe, body)

        @block.scalar
        def _(act):
            act.wait_ge(s["idx_ready"], 2)
            act.activation(sm[:, 12, :], sm[:, 11, :], ACT.Sin).then_inc(s["setup_act"], 1)
            act.wait_ge(s["setup_act"], 1)
            act.activation(sm[:, 13, :], sm[:, 12, :], ACT.Exp, scale=-1.0).then_inc(s["setup_act"], 1)
            act.wait_ge(s["setup_in"], 16 * SETUP_LOADS)
            act.wait_ge(s["setup_dve"], 2)
            act.wait_ge(s["u_zero"], 5)

            def body(i, attn, prev, nxt, pre, qkv, mid, ffn):
                a, c, m, f = i + 3, i + 2, i - 2, i - 3
                for t in range(TI):
                    if attn:
                        hh, qt = t // 4, t % 4
                        act.wait_ge(s["smax"], TI * i + t + 1)
                        tile = bias_s[:, hh % GH, qt, :]
                        act.activation(tile, tile, ACT.Exp, bias=mx[:, t:t + 1], scale=-1.0,
                                       accum_out=sums[:, t:t + 1]).then_inc(s["probs"], 1)

                    u = t - LAG
                    if (attn if u >= 0 else prev) and u % 2 == 1:
                        g = (u % TI) // 16
                        act.wait_ge(s["pt_ready"], TI * i + u + 1)
                        if u % 16 == 1:
                            wait(act, s["pv_done"], 2 * i + g - 1 if u >= 0 else 2 * i - 2)
                        act.copy(pT[g][:, (u // 4) % GH, :, (u % 4) * P:(u % 4 + 1) * P],
                                 tp[1][:, :].rearrange("p (k q) -> p k q", k=KT)).then_inc(s["copied_a"], 1)

                    if (attn if t >= 16 else prev) and t % 16 == CTXT_AT:
                        gi = 2 * i if t >= 16 else 2 * i - 1
                        act.wait_ge(s["pv_done"], gi + 1)
                        wait(act, s["ctxn_tr"], gi)
                        act.copy(cT[:, :], pv[:, :]).then_inc(s["ctxT_ready"], 1)

                    if pre and t == 4:
                        act.wait_ge(s["p_xt"], a + 1)
                        wait(act, s["p_down"], a)
                        act.copy(xT[:, :, :].rearrange("p c n -> p (c n)"), la[:, :]).then_inc(s["a_xt"], 1)
                    if pre and t == 12:
                        act.wait_ge(s["p_down"], a + 1)
                        act.activation(g_s[0:A, :], lb[0:A, 0:CH], ACT.Gelu,
                                       bias=vec[0:A, VEC["down_b"]:VEC["down_b"] + 1]).then_inc(s["a_gelu"], 1)
                    if pre and t == 16:
                        act.wait_ge(s["p_exp"], a + 1)
                        act.activation(h2[0:A, :], la[0:A, 0:CH], ACT.Identity, bias=ewx[0:A, A:A + 1]
                                       ).then_inc(s["a_h2"], 1)
                    if pre and t == 29:
                        act.wait_ge(s["p_xt1"], a + 1)
                        if qkv:
                            act.wait_ge(s["p_v"], c + 1)
                            act.wait_ge(s["p_k"], c + 1)
                        act.copy(xT1[:, :, :].rearrange("p c n -> p (c n)"), la[:, :]).then_inc(s["a_xt1"], 1)
                    if qkv and t == 2:
                        act.wait_ge(s["p_q"], c + 1)
                        wait(act, s["d_ks"], c)
                        for mt in range(2):
                            last = act.activation(qk[:, mt * CH:(mt + 1) * CH], lb[:, mt * CH:(mt + 1) * CH],
                                                  ACT.Identity, scale=-0.25, bias=nbq[:, mt:mt + 1])
                        last.then_inc(s["a_q"], 1)
                    if qkv and t == 13:
                        act.wait_ge(s["p_k"], c + 1)
                        act.wait_ge(s["d_qs"], c + 1)
                        for mt in range(2):
                            last = act.activation(qk[:, mt * CH:(mt + 1) * CH],
                                                  la[:, mt * CH:(mt + 1) * CH], ACT.Identity,
                                                  bias=vec[:, VEC["bk"] + mt:VEC["bk"] + mt + 1])
                        last.then_inc(s["a_k"], 1)

                    if ffn and t == 0:
                        act.wait_ge(s["p_ht"], f + 1)
                        for ct in range(CT):
                            last = act.activation(hT[:, ct, :], la[:, ct * CH:(ct + 1) * CH], ACT.Identity,
                                                  scale=vec[:, VEC["g2"] + ct:VEC["g2"] + ct + 1],
                                                  bias=vec[:, VEC["beta2"] + ct:VEC["beta2"] + ct + 1])
                        last.then_inc(s["a_hT"], 1)
                    if ffn and t in TANH_AT:
                        p = TANH_AT.index(t)
                        act.wait_ge(s["p_w1"], 4 * f + p + 1)
                        wait(act, s["d_act"], 4 * f + p)
                        for n in range(2):
                            last = act.activation(th[:, n * CH:(n + 1) * CH], w1_bank(p)[:, n * CH:(n + 1) * CH],
                                                  ACT.Tanh, scale=GATE, bias=b1g[:, 2 * p + n:2 * p + n + 1])
                        last.then_inc(s["a_th"], 1)

                    if mid and t == 21:
                        act.wait_ge(s["p_ct"], m + 1)
                        act.copy(cT2[:, :, :].rearrange("p c n -> p (c n)"), la[:, :]).then_inc(s["a_ct"], 1)

            each_iteration(act, body)

        @block.vector
        def _(dve):
            def link(chain, base, state, ins):
                state[0] += 1
                ins.then_inc(s[chain], 1)
                dve.wait_ge(s[chain], base + state[0])

            dve.memset(up_w[A:P, :], 0.0).then_inc(s["up_zero"], 1)
            for tile in (g_s, h2, ewx):
                dve.memset(tile[A:P, :], 0.0).then_inc(s["u_zero"], 1)
            dve.wait_ge(s["u_zero"], 5)
            dve.wait_ge(s["setup_in"], 16 * SETUP_LOADS)
            n = [0]
            su = lambda ins: link("setup_chain", 0, n, ins)
            su(dve.memset(h2[A:A + 1, :], 1.0))
            ef, ec, ok, bad = (sm[:, k, 0:B] for k in range(4))
            su(dve.tensor_copy(ef, e_i[:, :]))
            su(dve.tensor_scalar(ec, ef, 0.0, float(E - 1), ALU.max, ALU.min))
            su(dve.tensor_copy(idx_i[:, :], ec))
            dve.tensor_tensor(ok, ef, ec, ALU.is_equal).then_inc(s["idx_ready"], 1)
            dve.wait_ge(s["idx_ready"], 1)
            su(dve.tensor_scalar(bad, ok, -1.0, 1.0, ALU.mult, ALU.add))
            tf, q0, hi, lo, r, q1 = (sm[:, k, 0:B] for k in range(4, 10))
            inv100 = float(np.float32(1.0) / np.float32(100.0))
            su(dve.tensor_copy(tf, t_i[:, :]))
            su(dve.tensor_scalar(q0, tf, inv100, None, ALU.mult))
            su(dve.tensor_copy(tb[:, :], q0))
            su(dve.tensor_copy(hi, tb[:, :]))
            su(dve.tensor_tensor(lo, q0, hi, ALU.subtract))
            su(dve.scalar_tensor_tensor(out=r, in0=hi, scalar=-100.0, in1=tf, op0=ALU.mult, op1=ALU.add))
            su(dve.scalar_tensor_tensor(out=r, in0=lo, scalar=-100.0, in1=r, op0=ALU.mult, op1=ALU.add))
            su(dve.scalar_tensor_tensor(out=q1, in0=r, scalar=inv100, in1=q0, op0=ALU.mult, op1=ALU.add))
            su(dve.tensor_scalar(q1, q1, 4000.0, None, ALU.mult))
            arg, turn = sm[:, 10, :], sm[:, 14, :]
            freq = vec[:, VEC["freq"]:VEC["freq"] + 1]
            for j in range(2):
                su(dve.tensor_scalar(arg[:, j * B:(j + 1) * B], q1, freq, None, ALU.mult))
                su(dve.tensor_scalar(turn[:, j * B:(j + 1) * B], arg[:, j * B:(j + 1) * B],
                                     float(1 / TWO_PI), 0.25 * j, ALU.mult, ALU.add))
            su(dve.tensor_scalar(turn, turn, MAGIC, None, ALU.add))
            su(dve.tensor_scalar(turn, turn, MAGIC, None, ALU.subtract))
            for part in (C1, C2, C3):
                su(dve.scalar_tensor_tensor(out=arg, in0=turn, scalar=-part, in1=arg, op0=ALU.mult, op1=ALU.add))
            su(dve.tensor_scalar(arg[:, B:2 * B], arg[:, B:2 * B], float(np.pi / 2), None, ALU.add))
            dve.tensor_scalar(sm[:, 11, :], arg, -PI_IN, PI_IN, ALU.max, ALU.min).then_inc(s["idx_ready"], 1)
            dve.wait_ge(s["setup_act"], 2)
            su(dve.tensor_scalar(sm[:, 14, :], sm[:, 13, :], 1.0, None, ALU.add))
            su(dve.reciprocal(sm[:, 14, :], sm[:, 14, :]))
            su(dve.tensor_tensor(sm[:, 15, :], sm[:, 12, :], sm[:, 14, :], ALU.mult))
            dve.tensor_scalar(nbq[:, :], vec[:, 0:2], -0.25, None, ALU.mult)
            dve.tensor_scalar(b1g[:, :], vec[:, VEC["b1"]:VEC["b1"] + FT], GATE, None, ALU.mult)
            w2f = w2_s[:, :, :].rearrange("p c n -> p (c n)")
            su(dve.tensor_scalar(w2f, w2f, 0.5, None, ALU.mult))
            dve.wait_ge(s["expert_in"], 16 * 2 * B)
            okb = ok[0:A, :].unsqueeze(2).to_broadcast([A, B, A])
            badb = bad[0:A, :].unsqueeze(2).to_broadcast([A, B, A])
            su(dve.tensor_tensor(ew_all, ew_all, okb, ALU.mult))
            su(dve.tensor_tensor(ew_fin[:, :, 0:A], ident[0:A, 0:A].unsqueeze(1).to_broadcast([A, B, A]),
                                 badb, ALU.mult))
            su(dve.tensor_tensor(ew_fin[:, :, 0:A], ew_fin[:, :, 0:A], ew_all, ALU.add))
            su(dve.tensor_tensor(ebe[:, :, 0], ebe[:, :, 0], ok[0:A, :], ALU.mult))
            dve.tensor_tensor(ew_fin[:, :, A], ebe[:, :, 0], ebe[:, :, 1], ALU.add).then_inc(s["setup_dve"], 1)
            dve.wait_ge(s["setup_pe"], 1)
            su(dve.tensor_tensor(emb_s, lc[0:B, :], ada_r, ALU.add))
            dve.tensor_scalar(emb_s[:, 0:D], emb_s[:, 0:D], 1.0, None, ALU.add).then_inc(s["setup_dve"], 1)
            dve.wait_ge(s["setup_store"], 32)

            def body(i, attn, prev, nxt, pre, qkv, mid, ffn):
                a, c, m, f = i + 3, i + 2, i - 2, i - 3
                counts = dict(pre_chain=0, qkv_chain=0, mid_chain=0, ffn_chain=0)
                bases = dict(pre_chain=PRE_CHAIN * a, qkv_chain=QKV_CHAIN * c, mid_chain=MID_CHAIN * m,
                             ffn_chain=FFN_CHAIN * f)

                def step(chain, ins):
                    counts[chain] += 1
                    ins.then_inc(s[chain], 1)

                def after(chain):
                    dve.wait_ge(s[chain], bases[chain] + counts[chain])

                def row_stats(chain, rows_in, stats):
                    after(chain)
                    for j in range(2):
                        ins = dve.bn_stats(stats[:, j, :], rows_in[:, j, :])
                    step(chain, ins)

                def mean_var(chain, stats, mv, done):
                    after(chain)
                    apart(dve)
                    for j in range(2):
                        last = dve.bn_aggr(mv[:, j, :], stats[:, j, :])
                    last.then_inc(s[done], 1)

                def scaled(dst, rows_in, scalar, op0, other, op1):
                    for j in range(2):
                        last = dve.scalar_tensor_tensor(out=dst[:, j, :], in0=rows_in[:, j, :], scalar=scalar(j),
                                                        in1=other, op0=op0, op1=op1)
                    return last

                def add_rows(dst, psum, rows_in, done):
                    dve.tensor_tensor(dst[:, :, :].rearrange("p j n -> p (j n)"), psum[:, :],
                                      rows_in[:, :, :].rearrange("p j n -> p (j n)"), ALU.add
                                      ).then_inc(s[done], 1)

                def first_of_slot(t):
                    if ffn and t in GATE_AT:
                        p = GATE_AT.index(t)
                        dve.wait_ge(s["a_th"], 4 * f + p + 1)
                        step("ffn_chain", dve.tensor_scalar(th[:, :], th[:, :], 1.0, None, ALU.add))
                        after("ffn_chain")
                        if p == 0:
                            wait(dve, s["p_w2"], f)
                        for n in range(2):
                            ft = 2 * p + n
                            last = dve.scalar_tensor_tensor(
                                out=act_s[:, ft, :], in0=w1_bank(p)[:, n * CH:(n + 1) * CH],
                                scalar=vec[:, VEC["b1"] + ft:VEC["b1"] + ft + 1],
                                in1=th[:, n * CH:(n + 1) * CH], op0=ALU.add, op1=ALU.mult)
                        last.then_inc(s["d_act"], 1)
                    if pre and t == 20:
                        dve.wait_ge(s["d_x1"], a + 1)
                        row_stats("pre_chain", xin, st)
                    if pre and t == 21:
                        dve.wait_ge(s["d_mv0"], a + 1)
                        step("pre_chain", scaled(xin, xin, lambda j: mv0[:, j, 0:1], ALU.subtract,
                                                 gamma_r[:, :], ALU.mult))
                    if pre and t == 23:
                        row_stats("pre_chain", xin, st)
                    if pre and t == 24:
                        dve.wait_ge(s["d_mv1"], a + 1)
                        dve.wait_ge(s["mod_in"], 16 * (a + 1))
                        step("pre_chain", scaled(xin, xin, lambda j: mv1[:, j, 0:1], ALU.subtract,
                                                 mod[:, 0:D], ALU.mult))
                    if pre and t == 26:
                        dve.wait_ge(s["g_rs1"], a + 1)
                        after("pre_chain")
                        wait(dve, s["p_xt1"], a)
                        wait(dve, s["g_xs"], a)
                        scaled(xm, xin, lambda j: rs1[:, j:j + 1], ALU.mult, mod[:, D:2 * D], ALU.add
                               ).then_inc(s["d_xm"], 1)
                    if mid and t == 27:
                        mean_var("mid_chain", st2, mv2, "d_mv2")
                    if mid and t == 29:
                        dve.wait_ge(s["g_rs2"], m + 1)
                        for j in range(2):
                            last = dve.tensor_scalar(xsin[:, j, :], x2[:, j, :], mv2[:, j, 0:1], rs2[:, j:j + 1],
                                                     ALU.subtract, ALU.mult)
                        last.then_inc(s["d_hn"], 1)

                def last_of_slot(t):
                    if pre and t == 19:
                        dve.wait_ge(s["p_up"], a + 1)
                        add_rows(xin, lb, xin, "d_x1")
                    if pre and t == 20:
                        mean_var("pre_chain", st, mv0, "d_mv0")
                    if pre and t == 22:
                        dve.wait_ge(s["g_rs0"], a + 1)
                        after("pre_chain")
                        step("pre_chain", scaled(xin, xin, lambda j: rs0[:, j:j + 1], ALU.mult,
                                                 beta_r[:, :], ALU.add))
                    if pre and t == 23:
                        mean_var("pre_chain", st, mv1, "d_mv1")
                    if mid and t == 25:
                        dve.wait_ge(s["p_wo"], m + 1)
                        wait(dve, s["g_x2b"], m)
                        add_rows(x2, lb, xsin, "d_x2")
                    if mid and t == 26:
                        dve.wait_ge(s["d_x2"], m + 1)
                        row_stats("mid_chain", x2, st2)
                    if qkv and t == 7:
                        dve.wait_ge(s["p_v"], c + 1)
                        wait(dve, s["qkv_out"], 16 * QKV_STORES * c)
                        dve.tensor_tensor(vs[:, :, :], lb[:, :].rearrange("p (j n) -> p j n", j=2),
                                          bv_r[:, :].unsqueeze(1).to_broadcast([P, 2, D]), ALU.add
                                          ).then_inc(s["d_v"], 1)
                    if qkv and t in SPLIT_Q + SPLIT_K:
                        n = (SPLIT_Q + SPLIT_K).index(t)
                        off = 2 * CH * (n // 4)
                        part = [qkb[:, p, off:off + 2 * CH] for p in range(3)]
                        if n % 4 == 0:
                            dve.wait_ge(s["a_q" if n == 0 else "a_k"], c + 1)
                            wait(dve, s["qkv_out"], 16 * QKV_STORES * c)
                        else:
                            after("qkv_chain")
                        if n % 4 == 0:
                            step("qkv_chain", dve.tensor_copy(part[0], qk[:, :]))
                        elif n % 4 == 1:
                            step("qkv_chain", dve.tensor_tensor(qk[:, :], qk[:, :], part[0], ALU.subtract))
                        elif n % 4 == 2:
                            step("qkv_chain", dve.tensor_copy(part[1], qk[:, :]))
                        else:
                            dve.tensor_tensor(part[2], qk[:, :], part[1], ALU.subtract
                                              ).then_inc(s["d_qs" if n == 3 else "d_ks"], 1)
                    if ffn and t == 31:
                        dve.wait_ge(s["p_w2"], f + 1)
                        dve.wait_ge(s["g_x2b"], f + 1)
                        add_rows(x2b, lc, x2b, "d_out")

                for t in range(TI):
                    if attn:
                        hh, qt = t // 4, t % 4
                        dve.wait_ge(s["sc_ready"], TI * i + t + 1)
                        dve.wait_ge(s["masked"], 16 * i + 2 * hh + qt // 2 + 1)
                        apart(dve)
                        tile = bias_s[:, hh % GH, qt, :]
                        dve.tensor_tensor_reduce(out=tile, in0=sc[t % 2][:, :], in1=tile, scale=1.0, scalar=BIG,
                                                 op0=ALU.add, op1=ALU.min, accum_out=mx[:, t:t + 1]
                                                 ).then_inc(s["smax"], 1)
                    first_of_slot(t)

                    u = t - LAG
                    if (attn if u >= 0 else prev) and u % 2 == 0:
                        g = (u % TI) // 16
                        dve.wait_ge(s["pt_ready"], TI * i + u + 1)
                        if u % 16 == 0:
                            wait(dve, s["pv_done"], 2 * i + g - 1 if u >= 0 else 2 * i - 2)
                        dve.tensor_copy(pT[g][:, (u // 4) % GH, :, (u % 4) * P:(u % 4 + 1) * P],
                                        tp[0][:, :].rearrange("p (k q) -> p k q", k=KT)).then_inc(s["copied_v"], 1)

                    if (attn if t >= 16 else prev) and t % 16 == NORM_AT:
                        g = 0 if t >= 16 else 1
                        gi = 2 * i if t >= 16 else 2 * i - 1
                        dve.wait_ge(s["probs"], 16 * (gi + 1))
                        dve.reciprocal(rinv[:, :], sums[:, 16 * g:16 * g + 16]).then_inc(s["dve_rinv"], 1)
                        dve.wait_ge(s["dve_rinv"], gi + 1)
                        dve.wait_ge(s["ctxn_tr"], gi + 1)
                        wait(dve, ctx_out[g], 16 * (i - g))
                        dve.tensor_tensor(
                            cn[g][:, :, :].rearrange("p q (h d) -> p q h d", h=GH),
                            pv[:, :].rearrange("p (q h d) -> p q h d", q=KT, h=GH)[:, :, :, 0:HD],
                            rinv[:, :].rearrange("p (h q) -> p q h", q=KT).unsqueeze(3).to_broadcast(
                                [P, KT, GH, HD]), ALU.mult).then_inc(s["ctx_norm"], 1)
                    last_of_slot(t)
                for chain, on, n in (("pre_chain", pre, PRE_CHAIN), ("qkv_chain", qkv, QKV_CHAIN),
                                     ("mid_chain", mid, MID_CHAIN), ("ffn_chain", ffn, FFN_CHAIN)):
                    assert not on or counts[chain] == n, counts

            each_iteration(dve, body)


def kernel(**inputs):
    import concourse.bacc as bacc
    from concourse.bass_utils import run_bass_kernel_spmd

    def get(name):
        return np.asarray(inputs[name])

    def tiles(v, n):
        return v.reshape(n, P).T

    def by_head(w):
        return w.reshape(-1, 8, 2, HD).transpose(0, 2, 3, 1).reshape(-1, D)

    freqs = np.exp(np.arange(P, dtype=np.float32) * np.float32(-np.log(10000.0) / (P - 1))).astype(np.float32)
    down_b = np.concatenate([get("L0_cond_down_b"), np.zeros(P - A, np.float32)])
    vecs = np.concatenate([
        tiles(by_head(get("L1_cond_bq")[None])[0], 2), tiles(by_head(get("L1_cond_bk")[None])[0], 2),
        tiles(get("L1_cond_g2"), 2), tiles(get("L1_cond_beta2"), 2), tiles(get("L1_cond_b1"), FT),
        down_b[:, None], freqs[:, None]], axis=1)
    arrays = {
        "x": get("x").reshape(B * S, D),
        "t_tok": get("itok_B_34_63").reshape(1, B),
        "e_tok": get("itok_B_0_15").reshape(1, B),
        "bias": get("fside_Bx16xSxS_0").reshape(B * H, S, S),
        "mask": get("mask_Bx1xSxS_bk0").reshape(B, S, S),
        "downT": get("L0_cond_down_W").T,
        "upT": get("L0_cond_up_W").T,
        "up_b": get("L0_cond_up_b")[None],
        "expertT": get("L0_cond_expert_W").transpose(0, 2, 1),
        "expert_be": np.stack([get("L0_cond_expert_b"), get("L0_cond_domain_emb")], axis=2),
        "gamma": get("L0_cond_ln_gamma")[None],
        "beta": get("L0_cond_ln_beta")[None],
        "w_ada": get("L1_cond_W_ada"),
        "b_ada": get("L1_cond_b_ada")[None],
        "wq": by_head(get("L1_cond_Wq")),
        "wk": by_head(get("L1_cond_Wk")),
        "wv": get("L1_cond_Wv"),
        "bv": get("L1_cond_bv")[None],
        "wo": get("L1_cond_Wo"),
        "bo": get("L1_cond_bo")[None],
        "w1": get("L1_cond_W1"),
        "w2": get("L1_cond_W2"),
        "b2": get("L1_cond_b2")[None],
        "vecs": vecs,
        "ident_in": np.eye(P, dtype=np.float32),
    }
    nc = bacc.Bacc("TRN2", target_bir_lowering=False, num_devices=1)
    feed, aps = {}, {}
    for name, a in arrays.items():
        a = np.ascontiguousarray(a)
        feed[f"in_{name}"] = a
        aps[name] = nc.dram_tensor(f"in_{name}", a.shape, mybir.dt.from_np(a.dtype), kind="ExternalInput").ap()
    out = nc.dram_tensor("out_rows", (B * S, D), F32, kind="ExternalOutput").ap()
    build(nc, *aps.values(), out)
    got = run_bass_kernel_spmd(nc, [feed], core_ids=[0])
    return got.results[0]["out_rows"].reshape(B, S, D)
```

```python
from contextlib import ExitStack

import numpy as np

import concourse.bass as bass
from concourse import mybir

F32 = mybir.dt.float32
BF16 = mybir.dt.bfloat16
I32 = mybir.dt.int32
U8 = mybir.dt.uint8
ALU = mybir.AluOpType
ACT = mybir.ActivationFunctionType

P = 128
B, S, D = 8, 512, 256
H, HD = 16, 16
A, E = 64, 16
F = 1024
EPS = 1e-5
CH = 256
NCH = B * S // CH
CT = D // P
FT = F // P
GH = 4
TI = 32
KT = S // P
LAG = 4
MASKED = 1e30
BIG = 3.0e38
K_SLOTS = 5
RUNS = [(0, 3, 1), (48, 3, 2), (96, 2, 0)]
PE_AT = dict(q=(0.3, 2.3), v=(4.3, 5.3), down=6.6, exp=9.6, k=(13.6, 14.3), up=11.6, xt1=28.0,
             w1=(2.0, 5.6, 7.3, 9.6, 16.0, 16.3, 18.0, 20.3), w2=(20.6, 21.0, 25.0, 27.6, 27.6, 29.3, 30.3, 31.3),
             wo=(23.0, 26.3), ht=31.3, pv=((22.6, 24.0, 25.3, 27.0), (6.6, 7.0, 8.6, 10.3)), rinv=(29.6, 4.3))
ACT_AT = dict(hT=0.0, q=2.0, tanh=(5.3, 9.3, 17.3, 20.0), gelu=6.6, h2=9.0, k=16.0, xT1=28.0,
              cT=(27.3, 10.6))
DVE_AT = dict(q_split=(3.6, 7.0, 10.0, 11.0), gate=(7.0, 13.3, 19.6, 22.0), v=9.0, x1=16.0, st0=17.3,
              k_split=(18.3, 20.3, 23.0, 24.0), mv0=19.6, n1=21.6, n2=22.3, st1=23.0, mv1=23.6, m1=25.0,
              m2=26.3, x2=27.3, st2=27.6, mv2=28.0, hn=31.0, out=31.3, rinv=(20.0, 2.0), ctx=20.6,
              rinvT=(29.6, 4.6))
GATE = 1.702 / 2
FIRST, LAST = -3, NCH + 2
PRE_CHAIN, QKV_CHAIN, MID_CHAIN = 5, 6, 1
VEC = {"bq": 0, "bk": 2, "g2": 4, "beta2": 6, "b1": 8, "down_b": 16, "freq": 17}
TWO_PI = 2 * np.pi
C1 = 6.28125
C2 = float(np.round((TWO_PI - C1) * 2**21) / 2**21)
C3 = float(TWO_PI - C1 - C2)
MAGIC = 1.5 * 2.0**23
PI_IN = 3.1415925


def stages(i):
    return dict(attn=0 <= i < NCH, prev=1 <= i <= NCH, nxt=0 <= i + 1 < NCH, more=0 <= i + 4 < NCH,
                pre=0 <= i + 3 < NCH, qkv=0 <= i + 2 < NCH, mid=0 <= i - 2 < NCH, ffn=0 <= i - 3 < NCH)


def ahead(i):
    return isinstance(i, int) and i in (FIRST, FIRST + 1)


def wait(eng, sem, value):
    if isinstance(value, int) and value <= 0:
        return
    eng.wait_ge(sem, value)


def apart(eng):
    eng.nop(nofuse=True)


def each_iteration(eng, body):
    for i in range(FIRST, 3):
        body(i, **stages(i))
    with eng.Fori(3, NCH - 4) as i:
        body(i, **stages(3))
    for i in range(NCH - 4, LAST + 1):
        body(i, **stages(i))


def build(nc, x, x_t, t_tok, e_tok, bias, mask, downT, upT, up_b, experts, gamma, beta,
          w_ada, b_ada, wq, wk, wv, bv, wo, bo, w1, w2, b2, vecs, ident_in, out):
    x_v = x.rearrange("(c j p) d -> c p j d", j=2, p=P)
    xt_v = x_t.rearrange("(k p) (c t) -> c p k t", p=P, t=CH)
    out_v = out.rearrange("(c j p) d -> c p j d", j=2, p=P)
    bias_v = bias.rearrange("h (q p) k -> h p q k", p=P)
    mask_v = mask.rearrange("b (q p) k -> b p q k", p=P)

    def dram(name, shape, dt):
        return nc.dram_tensor(name, shape, dt, kind="Internal").ap()

    q_d = dram("q_parts", (B, H, 3 * HD, S), BF16)
    k_d = dram("k_parts", (B, H, K_SLOTS * HD, S), BF16)
    v_d = dram("v_rows", (B * S, D), F32)
    xs_d = dram("x_rows", (B * S, D), F32)
    ctx_d = dram("ctx_cols", (B, H, 2 * HD, S), F32)
    rinv_d = dram("row_sum_inverses", (B, H, S), F32)
    emb_d = dram("emb_rows", (B, 2 * D), F32)
    ew_d = dram("expert_rows", (B, A, A + 1), F32)
    xs_v = xs_d.rearrange("(c j p) d -> c p j d", j=2, p=P)
    v_v = v_d.rearrange("(c j p) d -> c p j d", j=2, p=P)
    v_b = v_d.rearrange("(b k p) d -> b p k d", k=KT, p=P)

    with ExitStack() as ctx:
        def sb(name, shape, dt=F32):
            return ctx.enter_context(nc.sbuf_tensor(name, shape, dt))

        def ps(name):
            return ctx.enter_context(nc.psum_tensor(name, [P, 512], F32))

        def sem(name):
            return ctx.enter_context(nc.semaphore(name))

        ident = sb("ident", [P, P])
        down_w = sb("down_w", [P, CT, A])
        up_w = sb("up_w", [P, D])
        wq_s = sb("wq_s", [P, CT, D])
        wk_s = sb("wk_s", [P, CT, D])
        wv_s = sb("wv_s", [P, CT, D])
        wo_s = sb("wo_s", [P, CT, D])
        w1_s = sb("w1_s", [P, CT, F])
        w2_s = sb("w2_s", [P, FT, D])
        gamma_r = sb("gamma_r", [P, D])
        beta_r = sb("beta_r", [P, D])
        bo_r = sb("bo_r", [P, D])
        bv_r = sb("bv_r", [P, D])
        b2_r = sb("b2_r", [P, D])
        vec = sb("vec", [P, 18])
        nbq = sb("nbq", [P, 2])
        b1g = sb("b1g", [P, FT])
        powc = sb("powc", [P, 2])

        bias_s = sb("bias_s", [P, GH, KT, S])
        mask_raw = sb("mask_raw", [P, KT, S], U8)
        mask_f = sb("mask_f", [P, KT, S])
        stq = [sb(f"stq{g}", [P, GH, S], BF16) for g in range(2)]
        stk = [sb(f"stk{g}", [P, GH, S], BF16) for g in range(2)]
        v_s = [sb(f"v_s{g}", [P, KT, GH * HD + HD]) for g in range(2)]
        pT = [sb(f"pT{g}", [P, GH, KT, S]) for g in range(2)]
        mx = sb("mx", [P, TI])
        sums = sb("sums", [P, TI])
        rinv = sb("rinv", [P, GH * KT])
        rinvT = sb("rinvT", [GH * KT, P])
        cT = sb("cT", [P, S])

        xin = sb("xin", [P, 2, D])
        xT = sb("xT", [P, CT, CH])
        xT1 = sb("xT1", [P, CT, CH])
        h2 = sb("h2", [P, CH])
        ewx = sb("ewx", [P, A + 1])
        mod = sb("mod", [P, 2 * D])
        xm = sb("xm", [P, 2, D])
        xs = sb("xs", [P, 2, D])
        qk = sb("qk", [P, 2 * CH])
        qkb = sb("qkb", [P, 3, 4 * CH], BF16)
        vs = sb("vs", [P, 2, D])
        st = sb("st", [P, 2, 6])
        mv0 = sb("mv0", [P, 2, 2])
        mv1 = sb("mv1", [P, 2, 2])
        rs0 = sb("rs0", [P, 2])
        rs1 = sb("rs1", [P, 2])

        cin = sb("cin", [P, CT, CH])
        rin = sb("rin", [P, CT, CH])
        xsin = sb("xsin", [P, 2, D])
        x2 = sb("x2", [P, 2, D])
        x2b = sb("x2b", [P, 2, D])
        hT = sb("hT", [P, CT, CH])
        st2 = sb("st2", [P, 2, 6])
        mv2 = sb("mv2", [P, 2, 2])
        rs2 = sb("rs2", [P, 2])
        th = sb("th", [P, 2 * CH])
        act_s = sb("act_s", [P, FT, CH])

        t_i = sb("t_i", [P, B], I32)
        e_i = sb("e_i", [P, B], I32)
        idx_i = sb("idx_i", [P, B], I32)
        tb = sb("tb", [P, B], BF16)
        sm = pT[0][:, 2, 2, 0:32 * B].rearrange("p (k n) -> p k n", n=2 * B)
        w_ada_s = pT[0][:, 0, 0:2, :]
        ew_all = pT[0][0:A, 1, 0:2, :].rearrange("p a n -> p (a n)")[:, 0:B * (A + 2)].rearrange(
            "p (b o) -> p b o", b=B)
        ew_fin = pT[0][0:A, 2, 0:2, :].rearrange("p a n -> p (a n)")[:, 0:B * (A + 1)].rearrange(
            "p (b o) -> p b o", b=B)
        ada_r = pT[0][0:B, 3, 0, :]
        emb_s = pT[0][0:B, 3, 1, :]

        sc = [ps("sc0"), ps("sc1")]
        tp = [ps("tp0"), ps("tp1")]
        pv = ps("pv")
        la, lb, lc = ps("la"), ps("lb"), ps("lc")

        def w1_bank(p, attn):
            return (lc, lc, lc, pv)[p] if attn else (lc, sc[0], sc[1], pv)[p]

        def tanh_of(p, attn):
            return th[:, :] if attn or p % 2 == 0 else xm[:, :, :].rearrange("p j n -> p (j n)")

        names = """
            setup_in first_in down_in ada_in qkv_w_in late_in up_zero u_zero setup_chain setup_dve
            setup_act setup_pe silu_ready idx_ready expert_in setup_store mask_in mask_ready masked
            sc_ready smax probs pt_ready copied_v copied_a pv_done ctxT_ready dve_rinv p_rinv
            rinvT_ready rinv_out x_in xt_in p_down a_gelu p_exp a_h2 p_up d_x1 d_mv0 g_rs0 mod_in ew_in
            d_mv1 g_rs1 d_xm p_xt1 a_xt1 p_q p_k a_q a_k d_qs d_ks p_v d_v g_xs xs_out qkv_out pre_chain
            pool_pre cx_in xs_in d_ctx p_wo d_x2 d_mv2 g_rs2 g_x2b d_hn p_ht a_hT mid_chain pool_mid
            p_w1 a_th d_act p_w2 d_out qkv_chain out_out""".split()
        s = {n: sem(n) for n in names}
        bias_in = [sem(f"bias_in{n}") for n in range(GH)]
        stack_in = [sem(f"stack_in{g}") for g in range(2)]
        v_in = [sem(f"v_in{g}") for g in range(2)]
        ctx_out = [sem(f"ctx_out{g}") for g in range(2)]
        FIRST_LOADS, SETUP_LOADS, QKV_W_LOADS, LATE_LOADS = 4, 4, 6, 3
        STACK_LOADS = 6
        QKV_STORES = 3 + K_SLOTS + 1

        block = ctx.enter_context(nc.Block())

        @block.sync
        def _(sp):
            def wait(eng, sem, value):
                if isinstance(value, int) and value <= 0:
                    return
                eng.wait_ge(sem, value)
                if not isinstance(value, int):
                    apart(eng)

            def load_bias(i, hh):
                wait(sp, s["pt_ready"], TI * i + 4 * hh - 12)
                sp.dma_start(bias_s[:, hh % GH, :, :],
                             bias_v[bass.ds(8 * i + hh, 1)].rearrange("h p q k -> (h p) q k")
                             ).then_inc(bias_in[hh % GH], 16)

            def load_mask(i):
                wait(sp, s["mask_ready"], i)
                sp.dma_start(mask_raw[:, :, :],
                             mask_v[bass.ds(i // 2, 1)].rearrange("b p q k -> (b p) q k")
                             ).then_inc(s["mask_in"], 16)

            def load_stack(i, g):
                head = (i % 2) * 8 + GH * g
                wait(sp, s["sc_ready"], TI * (i - 1) + 16 * (g + 1))
                for row, parts, k0 in RUNS:
                    n = parts * HD
                    qsrc = q_d[bass.ds(i // 2, 1), bass.ds(head, GH), 0:n, :]
                    ksrc = k_d[bass.ds(i // 2, 1), bass.ds(head, GH), k0 * HD:k0 * HD + n, :]
                    sp.dma_start(stq[g][row:row + n], qsrc.rearrange("b h r t -> (b r) h t")
                                 ).then_inc(stack_in[g], 16)
                    sp.dma_start(stk[g][row:row + n], ksrc.rearrange("b h r t -> (b r) h t")
                                 ).then_inc(stack_in[g], 16)

            def load_v(i, g):
                wait(sp, s["pv_done"], 2 * (i - 1) + g + 1)
                col = ((i % 2) * 8 + GH * g) * HD
                sp.dma_start(v_s[g][:, :, 0:GH * HD],
                             v_b[bass.ds(i // 2, 1), :, :, bass.ds(col, GH * HD)].rearrange(
                                 "b p k d -> (b p) k d")).then_inc(v_in[g], 16)

            def heads(view, i, g):
                return view[bass.ds(i // 2, 1), bass.ds((i % 2) * 8 + GH * g, GH)]

            def store_ctx(i, g):
                wait(sp, s["ctxT_ready"], 2 * i + g + 1)
                sp.dma_start(heads(ctx_d, i, g).rearrange("b h r t -> (b h r) t"), cT[:, :]
                             ).then_inc(ctx_out[g], 16)

            def store_rinv(i, g):
                wait(sp, s["rinvT_ready"], 2 * i + g + 1)
                sp.dma_start(heads(rinv_d, i, g).rearrange("b h (q t) -> (b h q) t", q=KT), rinvT[:, :]
                             ).then_inc(s["rinv_out"], 16)

            def load_ctx(m):
                wait(sp, s["p_wo"], m)
                for ct in range(CT):
                    at = (bass.ds(m // 2, 1), slice(8 * ct, 8 * ct + 8))
                    tok = bass.ds((m % 2) * CH, CH)
                    sp.dma_start(cin[:, ct, :], ctx_d[(*at, slice(0, HD), tok)].rearrange(
                        "b h r t -> (b h) r t")).then_inc(s["cx_in"], 16)
                    sp.dma_start(rin[:, ct, :], rinv_d[(*at, tok)].rearrange("b h t -> (b h) t").unsqueeze(
                        1).to_broadcast([8, HD, CH])).then_inc(s["cx_in"], 16)

            def rows(view, c):
                return view[bass.ds(c, 1)].rearrange("c p j d -> (c p) j d")

            def load_x(a):
                wait(sp, s["d_xm"], a)
                sp.dma_start(xin[:, :, :], rows(x_v, a)).then_inc(s["x_in"], 16)

            def load_xt(a):
                wait(sp, s["p_down"], a)
                sp.dma_start(xT[:, :, :], xt_v[bass.ds(a, 1)].rearrange("c p k t -> (c p) k t")
                             ).then_inc(s["xt_in"], 16)

            def load_expert(a):
                wait(sp, s["a_h2"], a)
                sp.dma_start(ewx[0:A, :], ew_d[bass.ds(a // 2, 1)].rearrange("b a o -> (b a) o")
                             ).then_inc(s["ew_in"], 16)

            def load_mod(a):
                wait(sp, s["d_xm"], a)
                sp.dma_start(mod[:, :], emb_d[bass.ds(a // 2, 1)].to_broadcast([P, 2 * D])
                             ).then_inc(s["mod_in"], 16)

            def load(sem_name, pairs):
                for dst, src in pairs:
                    sp.dma_start(dst, src).then_inc(s[sem_name], 16)

            load("first_in", [(t_i[:, :], t_tok.to_broadcast([P, B])), (e_i[:, :], e_tok.to_broadcast([P, B])),
                              (vec[:, :], vecs), (ident[:, :], ident_in)])
            load("xt_in", [(xT[:, :, :], xt_v[0])])
            load("down_in", [(down_w[:, :, :], downT.rearrange("(c p) a -> p c a", p=P))])
            load("ada_in", [(w_ada_s, w_ada.rearrange("(c p) n -> p c n", p=P)),
                            (ada_r, b_ada.to_broadcast([B, 2 * D]))])
            load("x_in", [(xin[:, :, :], x_v[0])])
            sp.wait_ge(s["idx_ready"], 1)
            for b in range(B):
                e = sp.value_load(idx_i[0:1, b:b + 1], min_val=0, max_val=E - 1)
                load("expert_in", [(ew_all[:, b, :], experts[bass.ds(e, 1)].rearrange("e a o -> (e a) o"))])
            sp.wait_ge(s["up_zero"], 1)
            load("setup_in", [(up_w[0:A, :], upT), (up_w[A:A + 1, :], up_b),
                              (gamma_r[:, :], gamma.to_broadcast([P, D])),
                              (beta_r[:, :], beta.to_broadcast([P, D]))])
            sp.wait_ge(s["setup_dve"], 1)
            load("ew_in", [(ewx[0:A, :], ew_fin[:, 0, :])])
            load("setup_store", [(ew_d.rearrange("b a o -> a b o"), ew_fin)])
            load_xt(1)
            load("qkv_w_in", [(wq_s[:, :, :], wq.rearrange("(c p) n -> p c n", p=P)),
                              (wk_s[:, :, :], wk.rearrange("(c p) n -> p c n", p=P)),
                              (wv_s[:, :, :], wv.rearrange("(c p) n -> p c n", p=P)),
                              (bo_r[:, :], bo.to_broadcast([P, D])), (bv_r[:, :], bv.to_broadcast([P, D])),
                              (b2_r[:, :], b2.to_broadcast([P, D]))])
            sp.wait_ge(s["setup_dve"], 2)
            load("setup_store", [(emb_d, emb_s)])
            sp.wait_ge(s["setup_store"], 32)
            load_mod(0)
            load_expert(1)
            load("late_in", [(wo_s[:, :, :], wo.rearrange("(c p) n -> p c n", p=P)),
                             (w1_s[:, :, :], w1.rearrange("(c p) n -> p c n", p=P)),
                             (w2_s[:, :, :], w2.rearrange("(c p) n -> p c n", p=P))])

            def store_parts(c, dst, slot, part, off):
                sp.dma_start(
                    dst[bass.ds(c // 2, 1), :, slot * HD:(slot + 1) * HD,
                        bass.ds((c % 2) * CH, CH)].rearrange("b h d t -> (b d) h t"),
                    qkb[:, part, off:off + 2 * CH].rearrange("p (m t) -> p m t", m=2)
                ).then_inc(s["qkv_out"], 16)

            def body(i, attn, prev, nxt, more, pre, qkv, mid, ffn):
                a, c, m, f = i + 3, i + 2, i - 2, i - 3
                if attn:
                    load_stack(i, 1)
                    load_bias(i, 3)
                if prev:
                    store_rinv(i - 1, 1)
                if attn:
                    load_bias(i, 4)
                    load_v(i, 1)
                if more and not (isinstance(i, int) and i == FIRST):
                    load_xt(a + 1)
                    load_expert(a + 1)
                if qkv:
                    wait(sp, s["d_qs"], c + 1)
                    for n in range(3):
                        store_parts(c, q_d, n, n, 0)
                if prev:
                    store_ctx(i - 1, 1)
                if attn:
                    load_bias(i, 5)
                if qkv:
                    wait(sp, s["d_v"], c + 1)
                    sp.dma_start(rows(v_v, c), vs[:, :, :]).then_inc(s["qkv_out"], 16)
                if ahead(i):
                    load_x(a + 1)
                if nxt:
                    load_mask(i + 1)
                if mid:
                    for g in range(2):
                        wait(sp, ctx_out[g], 16 * i if prev else 16 * NCH)
                    wait(sp, s["rinv_out"], 32 * i if prev else 32 * NCH)
                    wait(sp, s["xs_out"], 16 * (i + 3) if qkv else 16 * NCH)
                    load_ctx(m)
                    wait(sp, s["p_ht"], m)
                    sp.dma_start(xsin[:, :, :], rows(xs_v, m)).then_inc(s["xs_in"], 16)
                if attn:
                    load_bias(i, 6)
                    load_bias(i, 7)
                if nxt:
                    load_bias(i + 1, 0)
                if qkv:
                    wait(sp, s["d_ks"], c + 1)
                    for n in range(K_SLOTS):
                        store_parts(c, k_d, n, n % 3, 2 * CH)
                if nxt:
                    wait(sp, s["qkv_out"], 16 * QKV_STORES * (c + 1 if qkv else NCH))
                    load_stack(i + 1, 0)
                if nxt:
                    load_bias(i + 1, 1)
                if pre:
                    wait(sp, s["g_xs"], a + 1)
                    sp.dma_start(rows(xs_v, a), xs[:, :, :]).then_inc(s["xs_out"], 16)
                if more:
                    if not ahead(i):
                        load_x(a + 1)
                    load_mod(a + 1)
                if attn:
                    store_ctx(i, 0)
                if nxt:
                    load_v(i + 1, 0)
                    load_bias(i + 1, 2)
                if attn:
                    store_rinv(i, 0)
                if ffn:
                    wait(sp, s["d_out"], f + 1)
                    sp.dma_start(rows(out_v, f), x2b[:, :, :]).then_inc(s["out_out"], 16)

            each_iteration(sp, body)
            sp.wait_ge(s["out_out"], 16 * NCH)
            sp.wait_ge(s["xs_out"], 16 * NCH)
            sp.wait_ge(s["qkv_out"], 16 * QKV_STORES * NCH)
            for g in range(2):
                sp.wait_ge(ctx_out[g], 16 * NCH)
            sp.wait_ge(s["rinv_out"], 32 * NCH)

        @block.gpsimd
        def _(pool):
            pool.memset(powc[:, :], -0.5).then_inc(s["pool_pre"], 1)
            for g in range(2):
                pool.memset(v_s[g][:, :, :], 0.0).then_inc(s["u_zero"], 1)
            pool.wait_ge(s["pool_pre"], 1)
            pool.wait_ge(s["qkv_w_in"], 16 * QKV_W_LOADS)

            def mask_head(i, hh, halves=(0, 1)):
                if 0 in halves:
                    pool.wait_ge(bias_in[hh % GH], 16 * (2 * i + hh // GH + 1))
                for half in halves:
                    b = bias_s[:, hh % GH, 2 * half:2 * half + 2, :]
                    pool.tensor_tensor(b, mask_f[:, 2 * half:2 * half + 2, :], b, ALU.subtract
                                       ).then_inc(s["masked"], 1)

            def rsqrt(chain, base, var, dst):
                apart(pool)
                pool.tensor_scalar(dst, var, EPS, 1.0, ALU.add, ALU.mult).then_inc(s[chain], 1)
                pool.wait_ge(s[chain], base)
                return pool.tensor_tensor(dst, dst, powc[:, :], ALU.pow)

            def body(i, attn, prev, nxt, more, pre, qkv, mid, ffn):
                a, m, f = i + 3, i - 2, i - 3
                if attn:
                    mask_head(i, 1)
                    mask_head(i, 2)
                if ffn:
                    pool.wait_ge(s["d_x2"], f + 1)
                    wait(pool, s["out_out"], 16 * f)
                    pool.tensor_tensor(x2b[:, :, :], x2[:, :, :],
                                       b2_r[:, :].unsqueeze(1).to_broadcast([P, 2, D]), ALU.add
                                       ).then_inc(s["g_x2b"], 1)
                if attn:
                    for hh in range(3, 6):
                        mask_head(i, hh)
                if pre:
                    pool.wait_ge(s["d_mv0"], a + 1)
                    wait(pool, s["d_mv1"], a)
                    rsqrt("pool_pre", 2 * a + 2, mv0[:, :, 1], rs0[:, :]).then_inc(s["g_rs0"], 1)
                if attn:
                    mask_head(i, 6)
                    mask_head(i, 7)
                if pre:
                    pool.wait_ge(s["d_mv1"], a + 1)
                    wait(pool, s["d_xm"], a)
                    rsqrt("pool_pre", 2 * a + 3, mv1[:, :, 1], rs1[:, :]).then_inc(s["g_rs1"], 1)
                if nxt:
                    pool.wait_ge(s["mask_in"], 16 * (i + 2))
                    wait(pool, s["masked"], 16 * (i + 1))
                    apart(pool)
                    pool.tensor_scalar(mask_f[:, :, :], mask_raw[:, :, :], MASKED, 0.0, ALU.mult, ALU.add
                                       ).then_inc(s["mask_ready"], 1)
                    pool.wait_ge(s["mask_ready"], i + 2)
                    mask_head(i + 1, 0, (0,))
                if mid:
                    pool.wait_ge(s["d_mv2"], m + 1)
                    wait(pool, s["d_hn"], m)
                    rsqrt("pool_mid", m + 1, mv2[:, :, 1], rs2[:, :]).then_inc(s["g_rs2"], 1)
                if nxt:
                    mask_head(i + 1, 0, (1,))
                if pre:
                    pool.wait_ge(s["d_xm"], a + 1)
                    wait(pool, s["xs_out"], 16 * a)
                    pool.tensor_tensor(xs[:, :, :], xm[:, :, :],
                                       bo_r[:, :].unsqueeze(1).to_broadcast([P, 2, D]), ALU.add
                                       ).then_inc(s["g_xs"], 1)

            each_iteration(pool, body)

        @block.tensor
        def _(pe):
            def transposes(dst, src, done):
                for ct in range(CT):
                    for j in range(2):
                        last = pe.transpose(dst[:, ct * CH + j * P:ct * CH + (j + 1) * P],
                                            src[:, j, ct * P:(ct + 1) * P], ident[:, :])
                last.then_inc(s[done], 1)

            pe.wait_ge(s["first_in"], 16 * FIRST_LOADS)
            pe.wait_ge(s["u_zero"], 4)

            def embedding():
                pe.wait_ge(s["ada_in"], 32)
                pe.wait_ge(s["silu_ready"], 1)
                for j in range(2):
                    last = pe.matmul(lc[0:B, :], sm[:, 15, j * B:(j + 1) * B], w_ada_s[:, j, :],
                                     start=(j == 0), stop=(j == 1))
                last.then_inc(s["setup_pe"], 1)

            def adapter_down(a, f):
                if isinstance(a, int) and a == 0:
                    pe.wait_ge(s["down_in"], 16)
                pe.wait_ge(s["xt_in"], 16 * (a + 1))
                wait(pe, s["a_hT"], f + 1)
                for ct in range(CT):
                    last = pe.matmul(la[0:A, 0:CH], down_w[:, ct, :], xT[:, ct, :],
                                     start=(ct == 0), stop=(ct == CT - 1))
                last.then_inc(s["p_down"], 1)

            def adapter_expert(a):
                if isinstance(a, int) and a == 0:
                    embedding()
                pe.wait_ge(s["a_gelu"], a + 1)
                pe.wait_ge(s["ew_in"], 16 * (a + 1))
                pe.matmul(lb[0:A, 0:CH], ewx[:, 0:A], h2[:, :], start=True, stop=True
                          ).then_inc(s["p_exp"], 1)

            def adapter_up(a, bank):
                if isinstance(a, int) and a == 0:
                    pe.wait_ge(s["setup_in"], 16 * SETUP_LOADS)
                pe.wait_ge(s["a_h2"], a + 1)
                wait(pe, s["d_x1"], a)
                for j in range(2):
                    last = pe.matmul(bank[:, j * D:(j + 1) * D], h2[:, j * P:(j + 1) * P], up_w[:, :],
                                     start=True, stop=True)
                last.then_inc(s["p_up"], 1)

            def body(i, attn, prev, nxt, more, pre, qkv, mid, ffn):
                a, c, m, f = i + 3, i + 2, i - 2, i - 3
                AT = PE_AT

                def steps(t):
                    if qkv and t in AT["q"] + AT["k"]:
                        w, done, at = (wq_s, "p_q", AT["q"]) if t in AT["q"] else (wk_s, "p_k", AT["k"])
                        mt = at.index(t)
                        if t == AT["q"][0]:
                            pe.wait_ge(s["a_xt1"], c + 1)
                            wait(pe, s["d_x2"], m)
                        if t == AT["k"][0]:
                            pe.wait_ge(s["d_v"], c + 1)
                            wait(pe, s["a_h2"], a + 1 if pre else NCH)
                        for ct in range(CT):
                            last = pe.matmul(lb[:, mt * CH:(mt + 1) * CH], w[:, ct, mt * P:(mt + 1) * P],
                                             xT1[:, ct, :], start=(ct == 0), stop=(ct == CT - 1))
                        if mt == 1:
                            last.then_inc(s[done], 1)
                    if qkv and t in AT["v"]:
                        j = AT["v"].index(t)
                        if j == 0:
                            pe.wait_ge(s["a_q"], c + 1)
                        for ct in range(CT):
                            last = pe.matmul(lb[:, j * D:(j + 1) * D], xT1[:, ct, j * P:(j + 1) * P],
                                             wv_s[:, ct, :], start=(ct == 0), stop=(ct == CT - 1))
                        if j == 1:
                            last.then_inc(s["p_v"], 1)

                    own = pre and not ahead(i - 1)
                    if own and t == AT["down"]:
                        adapter_down(a, f)
                    if own and t == AT["exp"]:
                        wait(pe, s["d_v"], c + 1)
                        adapter_expert(a)
                    if own and t == AT["up"]:
                        adapter_up(a, la if attn else pv)
                    if ahead(i) and t == AT["xt1"]:
                        adapter_down(a + 1, f)
                        wait(pe, s["a_k"], c + 1)
                        adapter_expert(a + 1)
                        adapter_up(a + 1, pv)
                    if pre and t == AT["xt1"]:
                        pe.wait_ge(s["d_xm"], a + 1)
                        transposes(la, xm, "p_xt1")

                    if ffn and t in AT["w1"]:
                        ft = AT["w1"].index(t)
                        bank = w1_bank(ft // 2, attn)
                        if ft == 0:
                            pe.wait_ge(s["a_hT"], f + 1)
                            wait(pe, s["d_out"], f)
                        if ft == 2 and not attn:
                            pe.wait_ge(s["smax"], TI * NCH)
                        if ft in (2, 4) and attn:
                            pe.wait_ge(s["a_th"], 4 * f + ft // 2)
                        if ft == 6:
                            wait(pe, s["ctxT_ready"], 2 * i if prev else 2 * NCH)
                        for ct in range(CT):
                            last = pe.matmul(bank[:, (ft % 2) * CH:(ft % 2 + 1) * CH],
                                             w1_s[:, ct, ft * P:(ft + 1) * P],
                                             hT[:, ct, :], start=(ct == 0), stop=(ct == CT - 1))
                        if ft % 2 == 1:
                            last.then_inc(s["p_w1"], 1)
                    for r in range(8):
                        if ffn and t == AT["w2"][r]:
                            j = r // 4
                            if r == 0:
                                pe.wait_ge(s["a_th"], 4 * f + (3 if attn else 1))
                            if j == 0:
                                pe.wait_ge(s["d_act"], 4 * f + r + 1)
                            for ft in range(2 * (r % 4), 2 * (r % 4) + 2):
                                last = pe.matmul(lc[:, j * D:(j + 1) * D], act_s[:, ft, j * P:(j + 1) * P],
                                                 w2_s[:, ft, :], start=(ft == 0), stop=(ft == FT - 1))
                            if r == 7:
                                last.then_inc(s["p_w2"], 1)

                    if mid and t in AT["wo"]:
                        j = AT["wo"].index(t)
                        if j == 0:
                            pe.wait_ge(s["d_ctx"], m + 1)
                            if qkv:
                                pe.wait_ge(s["a_k"], c + 1)
                            else:
                                wait(pe, s["d_x2"], m)
                        for ct in range(CT):
                            last = pe.matmul(lb[:, j * D:(j + 1) * D], cin[:, ct, j * P:(j + 1) * P],
                                             wo_s[:, ct, :], start=(ct == 0), stop=(ct == CT - 1))
                        if j == 1:
                            last.then_inc(s["p_wo"], 1)
                    if mid and t == AT["ht"]:
                        pe.wait_ge(s["d_hn"], m + 1)
                        if pre:
                            pe.wait_ge(s["a_xt1"], a + 1)
                        transposes(la, xsin, "p_ht")

                    g = 0 if t >= 16 else 1
                    if (attn if g == 0 else prev) and t == AT["rinv"][g]:
                        gi = 2 * i - g
                        pe.wait_ge(s["dve_rinv"], gi + 1)
                        wait(pe, s["ctxT_ready"], gi + 1 - g)
                        pe.transpose(pv[0:GH * KT, 0:P], rinv[:, :], ident[:, :]).then_inc(s["p_rinv"], 1)

                    g = 0 if t >= 16 else 1
                    gi = 2 * i + g if g == 0 else 2 * i - 1
                    if (attn if g == 0 else prev) and t in AT["pv"][g]:
                        kt = AT["pv"][g].index(t)
                        if kt == 0:
                            pe.wait_ge(s["copied_v"], 8 * (gi + 1))
                            pe.wait_ge(s["copied_a"], 8 * (gi + 1))
                            pe.wait_ge(v_in[g], 16 * (i + 1 - g))
                            wait(pe, s["ctxT_ready"], gi)
                            wait(pe, s["rinvT_ready"], gi + g)
                            if ffn and g == 0:
                                pe.wait_ge(s["a_th"], 4 * f + 4)
                        for h in range(GH):
                            last = pe.matmul(pv[32 * h:32 * h + 32, :], v_s[g][:, kt, HD * h:HD * h + 32],
                                             pT[g][:, h, kt, :], start=(kt == 0), stop=(kt == KT - 1),
                                             tile_position=(0, 32 * h))
                        if kt == KT - 1:
                            last.then_inc(s["pv_done"], 1)

                if isinstance(i, int) and i == FIRST + 1:
                    pe.wait_ge(s["qkv_w_in"], 16 * QKV_W_LOADS)
                if isinstance(i, int) and i == 0:
                    pe.wait_ge(s["late_in"], 16 * LATE_LOADS)
                    pe.wait_ge(s["setup_dve"], 3)
                for t in range(TI):
                    steps(t)
                    if attn:
                        hh, qt = t // 4, t % 4
                        g = hh // GH
                        if t % 16 == 0:
                            pe.wait_ge(stack_in[g], 16 * STACK_LOADS * (i + 1))
                        wait(pe, s["smax"], TI * i + t - 1)
                        pe.matmul(sc[t % 2][:, :], stq[g][:, hh % GH, qt * P:(qt + 1) * P],
                                  stk[g][:, hh % GH, :], start=True, stop=True).then_inc(s["sc_ready"], 1)
                    steps(t + 0.3)

                    u = t - LAG
                    if attn if u >= 0 else prev:
                        pe.wait_ge(s["probs"], TI * i + u + 1)
                        wait(pe, s["copied_v" if u % 2 else "copied_a"], 16 * i + u // 2)
                        src = bias_s[:, (u // 4) % GH, u % 4, :]
                        for kt in range(KT):
                            last = pe.transpose(tp[u % 2][:, kt * P:(kt + 1) * P],
                                                src[:, kt * P:(kt + 1) * P], ident[:, :])
                        last.then_inc(s["pt_ready"], 1)
                    steps(t + 0.6)

            each_iteration(pe, body)

        @block.scalar
        def _(act):
            act.wait_ge(s["idx_ready"], 2)
            act.activation(sm[:, 12, :], sm[:, 11, :], ACT.Sin).then_inc(s["setup_act"], 1)
            act.wait_ge(s["setup_act"], 1)
            act.activation(sm[:, 13, :], sm[:, 12, :], ACT.Exp, scale=-1.0).then_inc(s["setup_act"], 1)
            act.wait_ge(s["first_in"], 16 * FIRST_LOADS)
            act.wait_ge(s["u_zero"], 4)

            def adapter_gelu(a):
                act.wait_ge(s["p_down"], a + 1)
                wait(act, s["p_up"], a)
                act.activation(h2[0:A, :], la[0:A, 0:CH], ACT.Gelu,
                               bias=vec[0:A, VEC["down_b"]:VEC["down_b"] + 1]).then_inc(s["a_gelu"], 1)

            def adapter_h2(a):
                act.wait_ge(s["p_exp"], a + 1)
                act.activation(h2[0:A, :], lb[0:A, 0:CH], ACT.Identity, bias=ewx[0:A, A:A + 1]
                               ).then_inc(s["a_h2"], 1)

            def body(i, attn, prev, nxt, more, pre, qkv, mid, ffn):
                a, c, m, f = i + 3, i + 2, i - 2, i - 3
                AT = ACT_AT

                def steps(t):
                    if ffn and t == AT["hT"]:
                        act.wait_ge(s["p_ht"], f + 1)
                        for ct in range(CT):
                            last = act.activation(hT[:, ct, :], la[:, ct * CH:(ct + 1) * CH], ACT.Identity,
                                                  scale=vec[:, VEC["g2"] + ct:VEC["g2"] + ct + 1],
                                                  bias=vec[:, VEC["beta2"] + ct:VEC["beta2"] + ct + 1])
                        last.then_inc(s["a_hT"], 1)

                    if pre and not ahead(i - 1) and t == AT["h2"]:
                        adapter_h2(a)

                    g = 0 if t >= 16 else 1
                    if (attn if g == 0 else prev) and t == AT["cT"][g]:
                        gi = 2 * i - g
                        act.wait_ge(s["pv_done"], gi + 1)
                        wait(act, ctx_out[1 - g], 16 * i)
                        act.copy(cT[:, :], pv[:, :]).then_inc(s["ctxT_ready"], 1)

                    if pre and not ahead(i - 1) and t == AT["gelu"]:
                        adapter_gelu(a)
                    if ahead(i) and t == AT["xT1"]:
                        adapter_gelu(a + 1)
                        adapter_h2(a + 1)
                    if pre and t == AT["xT1"]:
                        act.wait_ge(s["p_xt1"], a + 1)
                        if qkv:
                            act.wait_ge(s["p_v"], c + 1)
                            act.wait_ge(s["p_k"], c + 1)
                        act.copy(xT1[:, :, :].rearrange("p c n -> p (c n)"), la[:, :]).then_inc(s["a_xt1"], 1)
                    if qkv and t == AT["q"]:
                        act.wait_ge(s["p_q"], c + 1)
                        wait(act, s["d_ks"], c)
                        for mt in range(2):
                            last = act.activation(qk[:, mt * CH:(mt + 1) * CH], lb[:, mt * CH:(mt + 1) * CH],
                                                  ACT.Identity, scale=-0.25, bias=nbq[:, mt:mt + 1])
                        last.then_inc(s["a_q"], 1)
                    if qkv and t == AT["k"]:
                        act.wait_ge(s["p_k"], c + 1)
                        act.wait_ge(s["d_qs"], c + 1)
                        for mt in range(2):
                            last = act.activation(qk[:, mt * CH:(mt + 1) * CH],
                                                  lb[:, mt * CH:(mt + 1) * CH], ACT.Identity,
                                                  bias=vec[:, VEC["bk"] + mt:VEC["bk"] + mt + 1])
                        last.then_inc(s["a_k"], 1)

                    if ffn and t in AT["tanh"]:
                        p = AT["tanh"].index(t)
                        act.wait_ge(s["p_w1"], 4 * f + p + 1)
                        wait(act, s["d_act"], 4 * f + p - (0 if attn else 1))
                        if p == 0:
                            wait(act, s["p_w2"], f)
                        for n in range(2):
                            ft = 2 * p + n
                            h = w1_bank(p, attn)[:, n * CH:(n + 1) * CH]
                            act.activation(tanh_of(p, attn)[:, n * CH:(n + 1) * CH], h,
                                           ACT.Tanh, scale=GATE, bias=b1g[:, ft:ft + 1])
                            last = act.activation(act_s[:, ft, :], h, ACT.Identity,
                                                  bias=vec[:, VEC["b1"] + ft:VEC["b1"] + ft + 1])
                        last.then_inc(s["a_th"], 1)

                if isinstance(i, int) and i == FIRST + 1:
                    act.wait_ge(s["setup_dve"], 2)
                if isinstance(i, int) and i == 0:
                    act.wait_ge(s["setup_dve"], 3)
                for t in range(TI):
                    steps(t)
                    if attn:
                        hh, qt = t // 4, t % 4
                        act.wait_ge(s["smax"], TI * i + t + 1)
                        tile = bias_s[:, hh % GH, qt, :]
                        act.activation(tile, tile, ACT.Exp, bias=mx[:, t:t + 1], scale=-1.0,
                                       accum_out=sums[:, t:t + 1]).then_inc(s["probs"], 1)

                    steps(t + 0.3)
                    u = t - LAG
                    if (attn if u >= 0 else prev) and u % 2 == 0:
                        g = (u % TI) // 16
                        act.wait_ge(s["pt_ready"], TI * i + u + 1)
                        if u % 16 == 0:
                            wait(act, s["pv_done"], 2 * i + g - 1 if u >= 0 else 2 * i - 2)
                        act.copy(pT[g][:, (u // 4) % GH, :, (u % 4) * P:(u % 4 + 1) * P],
                                 tp[0][:, :].rearrange("p (k q) -> p k q", k=KT)).then_inc(s["copied_a"], 1)
                    steps(t + 0.6)

            each_iteration(act, body)

        @block.vector
        def _(dve):
            def link(chain, base, state, ins):
                state[0] += 1
                ins.then_inc(s[chain], 1)
                dve.wait_ge(s[chain], base + state[0])

            dve.memset(up_w[A:P, :], 0.0).then_inc(s["up_zero"], 1)
            for tile in (h2, ewx):
                dve.memset(tile[A:P, :], 0.0).then_inc(s["u_zero"], 1)
            dve.wait_ge(s["u_zero"], 4)
            dve.wait_ge(s["first_in"], 16 * FIRST_LOADS)
            n = [0]
            su = lambda ins: link("setup_chain", 0, n, ins)
            su(dve.memset(h2[A:A + 1, :], 1.0))
            ef, ec, ok, bad = (sm[:, k, 0:B] for k in range(4))
            su(dve.tensor_copy(ef, e_i[:, :]))
            su(dve.tensor_scalar(ec, ef, 0.0, float(E - 1), ALU.max, ALU.min))
            su(dve.tensor_copy(idx_i[:, :], ec))
            dve.tensor_tensor(ok, ef, ec, ALU.is_equal).then_inc(s["idx_ready"], 1)
            dve.wait_ge(s["idx_ready"], 1)
            su(dve.tensor_scalar(bad, ok, -1.0, 1.0, ALU.mult, ALU.add))
            tf, q0, hi, lo, r, q1 = (sm[:, k, 0:B] for k in range(4, 10))
            inv100 = float(np.float32(1.0) / np.float32(100.0))
            su(dve.tensor_copy(tf, t_i[:, :]))
            su(dve.tensor_scalar(q0, tf, inv100, None, ALU.mult))
            su(dve.tensor_copy(tb[:, :], q0))
            su(dve.tensor_copy(hi, tb[:, :]))
            su(dve.tensor_tensor(lo, q0, hi, ALU.subtract))
            su(dve.scalar_tensor_tensor(out=r, in0=hi, scalar=-100.0, in1=tf, op0=ALU.mult, op1=ALU.add))
            su(dve.scalar_tensor_tensor(out=r, in0=lo, scalar=-100.0, in1=r, op0=ALU.mult, op1=ALU.add))
            su(dve.scalar_tensor_tensor(out=q1, in0=r, scalar=inv100, in1=q0, op0=ALU.mult, op1=ALU.add))
            su(dve.tensor_scalar(q1, q1, 4000.0, None, ALU.mult))
            arg, turn = sm[:, 10, :], sm[:, 14, :]
            freq = vec[:, VEC["freq"]:VEC["freq"] + 1]
            for j in range(2):
                su(dve.tensor_scalar(arg[:, j * B:(j + 1) * B], q1, freq, None, ALU.mult))
                su(dve.tensor_scalar(turn[:, j * B:(j + 1) * B], arg[:, j * B:(j + 1) * B],
                                     float(1 / TWO_PI), 0.25 * j, ALU.mult, ALU.add))
            su(dve.tensor_scalar(turn, turn, MAGIC, None, ALU.add))
            su(dve.tensor_scalar(turn, turn, MAGIC, None, ALU.subtract))
            for part in (C1, C2, C3):
                su(dve.scalar_tensor_tensor(out=arg, in0=turn, scalar=-part, in1=arg, op0=ALU.mult, op1=ALU.add))
            su(dve.tensor_scalar(arg[:, B:2 * B], arg[:, B:2 * B], float(np.pi / 2), None, ALU.add))
            dve.tensor_scalar(sm[:, 11, :], arg, -PI_IN, PI_IN, ALU.max, ALU.min).then_inc(s["idx_ready"], 1)
            dve.wait_ge(s["setup_act"], 2)
            su(dve.tensor_scalar(sm[:, 14, :], sm[:, 13, :], 1.0, None, ALU.add))
            su(dve.reciprocal(sm[:, 14, :], sm[:, 14, :]))
            dve.tensor_tensor(sm[:, 15, :], sm[:, 12, :], sm[:, 14, :], ALU.mult).then_inc(s["silu_ready"], 1)
            dve.tensor_scalar(nbq[:, :], vec[:, 0:2], -0.25, None, ALU.mult)
            dve.tensor_scalar(b1g[:, :], vec[:, VEC["b1"]:VEC["b1"] + FT], GATE, None, ALU.mult)
            dve.wait_ge(s["expert_in"], 16 * B)
            okb = ok[0:A, :].unsqueeze(2).to_broadcast([A, B, A + 1])
            badb = bad[0:A, :].unsqueeze(2).to_broadcast([A, B, A])
            su(dve.tensor_tensor(ew_all[:, :, 0:A + 1], ew_all[:, :, 0:A + 1], okb, ALU.mult))
            su(dve.tensor_tensor(ew_fin[:, :, 0:A], ident[0:A, 0:A].unsqueeze(1).to_broadcast([A, B, A]),
                                 badb, ALU.mult))
            dve.tensor_tensor(ew_fin[:, :, 0:A], ew_fin[:, :, 0:A], ew_all[:, :, 0:A], ALU.add)
            dve.tensor_tensor(ew_fin[:, :, A], ew_all[:, :, A], ew_all[:, :, A + 1], ALU.add).then_inc(s["setup_dve"], 1)
            dve.wait_ge(s["setup_pe"], 1)
            su(dve.tensor_tensor(emb_s, lc[0:B, :], ada_r, ALU.add))
            dve.tensor_scalar(emb_s[:, 0:D], emb_s[:, 0:D], 1.0, None, ALU.add).then_inc(s["setup_dve"], 1)
            dve.wait_ge(s["setup_in"], 16 * SETUP_LOADS)

            def body(i, attn, prev, nxt, more, pre, qkv, mid, ffn):
                a, c, m, f = i + 3, i + 2, i - 2, i - 3
                AT = DVE_AT
                early = int(AT["x1"]) if isinstance(i, int) and i == -1 else 0
                norm_at = {n: round(AT[n] - early, 1) for n in ("x1", "st0", "mv0", "n1", "n2", "st1", "mv1",
                                                                "m1", "m2")}
                counts = dict(pre_chain=0, qkv_chain=0, mid_chain=0)
                bases = dict(pre_chain=PRE_CHAIN * a, qkv_chain=QKV_CHAIN * c, mid_chain=MID_CHAIN * m,
                             )

                def step(chain, ins):
                    counts[chain] += 1
                    ins.then_inc(s[chain], 1)

                def after(chain):
                    dve.wait_ge(s[chain], bases[chain] + counts[chain])

                def row_stats(chain, rows_in, stats):
                    after(chain)
                    for j in range(2):
                        ins = dve.bn_stats(stats[:, j, :], rows_in[:, j, :])
                    step(chain, ins)

                def mean_var(chain, stats, mv, done):
                    after(chain)
                    apart(dve)
                    for j in range(2):
                        last = dve.bn_aggr(mv[:, j, :], stats[:, j, :])
                    last.then_inc(s[done], 1)

                def scaled(dst, rows_in, scalar, op0, other, op1):
                    for j in range(2):
                        last = dve.scalar_tensor_tensor(out=dst[:, j, :], in0=rows_in[:, j, :], scalar=scalar(j),
                                                        in1=other, op0=op0, op1=op1)
                    return last

                def add_rows(dst, psum, rows_in, done):
                    dve.tensor_tensor(dst[:, :, :].rearrange("p j n -> p (j n)"), psum[:, :],
                                      rows_in[:, :, :].rearrange("p j n -> p (j n)"), ALU.add
                                      ).then_inc(s[done], 1)

                def steps(t):
                    g = 0 if t >= 16 else 1
                    if (attn if g == 0 else prev) and t == AT["rinv"][g]:
                        gi = 2 * i - g
                        dve.wait_ge(s["probs"], 16 * (gi + 1))
                        wait(dve, s["p_rinv"], gi)
                        dve.reciprocal(rinv[:, :], sums[:, 16 * g:16 * g + 16]).then_inc(s["dve_rinv"], 1)
                    if (attn if g == 0 else prev) and t == AT["rinvT"][g]:
                        gi = 2 * i - g
                        dve.wait_ge(s["p_rinv"], gi + 1)
                        wait(dve, s["rinv_out"], 16 * gi)
                        dve.tensor_copy(rinvT[:, :], pv[0:GH * KT, 0:P]).then_inc(s["rinvT_ready"], 1)
                    if mid and t == AT["ctx"]:
                        dve.wait_ge(s["cx_in"], 64 * (m + 1))
                        dve.tensor_tensor(cin[:, :, :], cin[:, :, :], rin[:, :, :], ALU.mult
                                          ).then_inc(s["d_ctx"], 1)
                    if ffn and t in AT["gate"]:
                        p = AT["gate"].index(t)
                        dve.wait_ge(s["a_th"], 4 * f + p + 1)
                        u = act_s[:, 2 * p:2 * p + 2, :].rearrange("p c n -> p (c n)")
                        dve.scalar_tensor_tensor(out=u, in0=tanh_of(p, attn), scalar=1.0, in1=u,
                                                 op0=ALU.add, op1=ALU.mult).then_inc(s["d_act"], 1)
                    if pre and t == norm_at["st0"]:
                        dve.wait_ge(s["d_x1"], a + 1)
                        row_stats("pre_chain", xin, st)
                    if pre and t == norm_at["n1"]:
                        dve.wait_ge(s["d_mv0"], a + 1)
                        step("pre_chain", scaled(xin, xin, lambda j: mv0[:, j, 0:1], ALU.subtract,
                                                 gamma_r[:, :], ALU.mult))
                    if pre and t == norm_at["st1"]:
                        row_stats("pre_chain", xin, st)
                    if pre and t == norm_at["m2"]:
                        dve.wait_ge(s["g_rs1"], a + 1)
                        after("pre_chain")
                        wait(dve, s["p_xt1"], a)
                        wait(dve, s["g_xs"], a)
                        scaled(xm, xin, lambda j: rs1[:, j:j + 1], ALU.mult, mod[:, D:2 * D], ALU.add
                               ).then_inc(s["d_xm"], 1)
                    if mid and t == AT["mv2"]:
                        mean_var("mid_chain", st2, mv2, "d_mv2")
                    if mid and t == AT["hn"]:
                        dve.wait_ge(s["g_rs2"], m + 1)
                        for j in range(2):
                            last = dve.tensor_scalar(xsin[:, j, :], x2[:, j, :], mv2[:, j, 0:1], rs2[:, j:j + 1],
                                                     ALU.subtract, ALU.mult)
                        last.then_inc(s["d_hn"], 1)

                    if pre and t == norm_at["x1"]:
                        dve.wait_ge(s["p_up"], a + 1)
                        dve.wait_ge(s["x_in"], 16 * (a + 1))
                        add_rows(xin, la if attn else pv, xin, "d_x1")
                    if pre and t == norm_at["mv0"]:
                        mean_var("pre_chain", st, mv0, "d_mv0")
                    if pre and t == norm_at["n2"]:
                        dve.wait_ge(s["g_rs0"], a + 1)
                        after("pre_chain")
                        step("pre_chain", scaled(xin, xin, lambda j: rs0[:, j:j + 1], ALU.mult,
                                                 beta_r[:, :], ALU.add))
                    if pre and t == norm_at["mv1"]:
                        mean_var("pre_chain", st, mv1, "d_mv1")
                    if mid and t == AT["x2"]:
                        dve.wait_ge(s["p_wo"], m + 1)
                        dve.wait_ge(s["xs_in"], 16 * (m + 1))
                        wait(dve, s["g_x2b"], m)
                        add_rows(x2, lb, xsin, "d_x2")
                    if pre and t == norm_at["m1"]:
                        dve.wait_ge(s["d_mv1"], a + 1)
                        dve.wait_ge(s["mod_in"], 16 * (a + 1))
                        step("pre_chain", scaled(xin, xin, lambda j: mv1[:, j, 0:1], ALU.subtract,
                                                 mod[:, 0:D], ALU.mult))
                    if mid and t == AT["st2"]:
                        dve.wait_ge(s["d_x2"], m + 1)
                        row_stats("mid_chain", x2, st2)
                    if qkv and t == AT["v"]:
                        dve.wait_ge(s["p_v"], c + 1)
                        wait(dve, s["qkv_out"], 16 * QKV_STORES * c)
                        dve.tensor_tensor(vs[:, :, :], lb[:, :].rearrange("p (j n) -> p j n", j=2),
                                          bv_r[:, :].unsqueeze(1).to_broadcast([P, 2, D]), ALU.add
                                          ).then_inc(s["d_v"], 1)
                    splits = AT["q_split"] + AT["k_split"]
                    if qkv and t in splits:
                        n = splits.index(t)
                        off = 2 * CH * (n // 4)
                        part = [qkb[:, p, off:off + 2 * CH] for p in range(3)]
                        if n % 4 == 0:
                            dve.wait_ge(s["a_q" if n == 0 else "a_k"], c + 1)
                            wait(dve, s["qkv_out"], 16 * QKV_STORES * c)
                        else:
                            after("qkv_chain")
                        if n % 4 == 0:
                            step("qkv_chain", dve.tensor_copy(part[0], qk[:, :]))
                        elif n % 4 == 1:
                            step("qkv_chain", dve.tensor_tensor(qk[:, :], qk[:, :], part[0], ALU.subtract))
                        elif n % 4 == 2:
                            step("qkv_chain", dve.tensor_copy(part[1], qk[:, :]))
                        else:
                            dve.tensor_tensor(part[2], qk[:, :], part[1], ALU.subtract
                                              ).then_inc(s["d_qs" if n == 3 else "d_ks"], 1)
                    if ffn and t == AT["out"]:
                        dve.wait_ge(s["p_w2"], f + 1)
                        dve.wait_ge(s["g_x2b"], f + 1)
                        add_rows(x2b, lc, x2b, "d_out")

                if isinstance(i, int) and i == FIRST + 1:
                    dve.wait_ge(s["qkv_w_in"], 16 * QKV_W_LOADS)
                if isinstance(i, int) and i == -1:
                    dve.wait_ge(s["late_in"], 16 * LATE_LOADS)
                    w2f = w2_s[:, :, :].rearrange("p c n -> p (c n)")
                    dve.tensor_scalar(w2f, w2f, 0.5, None, ALU.mult).then_inc(s["setup_dve"], 1)
                    dve.wait_ge(s["setup_store"], 32)
                for t in range(TI):
                    steps(t)
                    if attn:
                        hh, qt = t // 4, t % 4
                        dve.wait_ge(s["sc_ready"], TI * i + t + 1)
                        dve.wait_ge(s["masked"], 16 * i + 2 * hh + qt // 2 + 1)
                        apart(dve)
                        tile = bias_s[:, hh % GH, qt, :]
                        dve.tensor_tensor_reduce(out=tile, in0=sc[t % 2][:, :], in1=tile, scale=1.0, scalar=BIG,
                                                 op0=ALU.add, op1=ALU.min, accum_out=mx[:, t:t + 1]
                                                 ).then_inc(s["smax"], 1)
                    steps(t + 0.3)

                    u = t - LAG
                    if (attn if u >= 0 else prev) and u % 2 == 1:
                        g = (u % TI) // 16
                        dve.wait_ge(s["pt_ready"], TI * i + u + 1)
                        if u % 16 == 1:
                            wait(dve, s["pv_done"], 2 * i + g - 1 if u >= 0 else 2 * i - 2)
                        dve.tensor_copy(pT[g][:, (u // 4) % GH, :, (u % 4) * P:(u % 4 + 1) * P],
                                        tp[1][:, :].rearrange("p (k q) -> p k q", k=KT)).then_inc(s["copied_v"], 1)

                    steps(t + 0.6)
                for chain, on, n in (("pre_chain", pre, PRE_CHAIN), ("qkv_chain", qkv, QKV_CHAIN),
                                     ("mid_chain", mid, MID_CHAIN),):
                    assert not on or counts[chain] == n, counts

            each_iteration(dve, body)


def kernel(**inputs):
    import concourse.bacc as bacc
    from concourse.bass_utils import run_bass_kernel_spmd

    def get(name):
        return np.asarray(inputs[name])

    def tiles(v, n):
        return v.reshape(n, P).T

    def by_head(w):
        return w.reshape(-1, 8, 2, HD).transpose(0, 2, 3, 1).reshape(-1, D)

    freqs = np.exp(np.arange(P, dtype=np.float32) * np.float32(-np.log(10000.0) / (P - 1))).astype(np.float32)
    down_b = np.concatenate([get("L0_cond_down_b"), np.zeros(P - A, np.float32)])
    vecs = np.concatenate([
        tiles(by_head(get("L1_cond_bq")[None])[0], 2), tiles(by_head(get("L1_cond_bk")[None])[0], 2),
        tiles(get("L1_cond_g2"), 2), tiles(get("L1_cond_beta2"), 2), tiles(get("L1_cond_b1"), FT),
        down_b[:, None], freqs[:, None]], axis=1)
    arrays = {
        "x": get("x").reshape(B * S, D),
        "x_t": get("x").reshape(B * S, D).T,
        "t_tok": get("itok_B_34_63").reshape(1, B),
        "e_tok": get("itok_B_0_15").reshape(1, B),
        "bias": get("fside_Bx16xSxS_0").reshape(B * H, S, S),
        "mask": get("mask_Bx1xSxS_bk0").reshape(B, S, S),
        "downT": get("L0_cond_down_W").T,
        "upT": get("L0_cond_up_W").T,
        "up_b": get("L0_cond_up_b")[None],
        "experts": np.concatenate([get("L0_cond_expert_W").transpose(0, 2, 1),
                                   get("L0_cond_expert_b")[:, :, None],
                                   get("L0_cond_domain_emb")[:, :, None]], axis=2),
        "gamma": get("L0_cond_ln_gamma")[None],
        "beta": get("L0_cond_ln_beta")[None],
        "w_ada": get("L1_cond_W_ada"),
        "b_ada": get("L1_cond_b_ada")[None],
        "wq": by_head(get("L1_cond_Wq")),
        "wk": by_head(get("L1_cond_Wk")),
        "wv": get("L1_cond_Wv"),
        "bv": get("L1_cond_bv")[None],
        "wo": get("L1_cond_Wo"),
        "bo": get("L1_cond_bo")[None],
        "w1": get("L1_cond_W1"),
        "w2": get("L1_cond_W2"),
        "b2": get("L1_cond_b2")[None],
        "vecs": vecs,
        "ident_in": np.eye(P, dtype=np.float32),
    }
    nc = bacc.Bacc("TRN2", target_bir_lowering=False, num_devices=1)
    feed, aps = {}, {}
    for name, a in arrays.items():
        a = np.ascontiguousarray(a)
        feed[f"in_{name}"] = a
        aps[name] = nc.dram_tensor(f"in_{name}", a.shape, mybir.dt.from_np(a.dtype), kind="ExternalInput").ap()
    out = nc.dram_tensor("out_rows", (B * S, D), F32, kind="ExternalOutput").ap()
    build(nc, *aps.values(), out)
    got = run_bass_kernel_spmd(nc, [feed], core_ids=[0])
    return got.results[0]["out_rows"].reshape(B, S, D)
```
